# Optimizing a Trainium2 kernel written in Bass

```python
import numpy as np
import jax
import jax.numpy as jnp

def _softmax(x, axis=-1):
    return jax.nn.softmax(x, axis=axis)

def _gelu(x):
    return jax.nn.gelu(x, approximate=True)

def _silu(x):
    return jax.nn.silu(x)

def _sigmoid(x):
    return jax.nn.sigmoid(x)

def _layernorm(x, axis=-1, eps=1e-05):
    m = jnp.mean(x, axis=axis, keepdims=True)
    v = jnp.var(x, axis=axis, keepdims=True)
    return (x - m) / jnp.sqrt(v + eps)

def _scatter_add(tgt, idx, src, axis=0):
    return tgt.at[idx].add(src)

def _segment_sum(src, seg, n):
    return jax.ops.segment_sum(src, seg, n)
kernel_name = 'mk_cond_seq_d2_seqx_r2_cb07d2'

def setup_inputs(seed: int=0):
    np.random.seed(seed)
    _w = jnp.asarray

    def _rec_inputs():
        import jax
        import jax.numpy as jnp
        _rk = jax.random.key(seed)
        x = -0.0003929 + 0.9999 * jax.random.normal(jax.random.fold_in(_rk, 1), (32, 128, 512), jnp.float32)
        _lenS = 128 - jax.random.randint(jax.random.fold_in(_rk, 7), (32,), 0, max(1, 128 // 4) + 1, jnp.int32)
        _lenS2 = 128 - jax.random.randint(jax.random.fold_in(_rk, 8), (32,), 0, max(1, 128 // 4) + 1, jnp.int32)
        cond_2048 = 0.00782532 + 1.00527 * jax.random.normal(jax.random.fold_in(_rk, 11), (32, 1024), jnp.float32)
        _validS = jnp.arange(128)[None, :] < _lenS[:, None]
        _validS2 = jnp.arange(128)[None, :] < _lenS2[:, None]
        _causal = jnp.tril(jnp.ones((128, 128), dtype=bool))
        mask_BxS_ik0 = jnp.where(jnp.broadcast_to(_validS[:, :], (32, 128)), 0, 1).astype(jnp.int32)
        mask_BxSx1_fk1 = jnp.where(jnp.ones((32, 128, 1), dtype=bool), 1.0, 0.0).astype(jnp.float32)
        return (x, cond_2048, mask_BxS_ik0, mask_BxSx1_fk1)
    x, cond_2048, mask_BxS_ik0, mask_BxSx1_fk1 = _rec_inputs()

    def _L0_cond_setup():
        import jax, jax.numpy as jnp
        import numpy as np
        H = 16
        LN_EPS = 1e-05

        def _layernorm(x, scale, bias):
            mu = jnp.mean(x, axis=-1, keepdims=True)
            var = jnp.var(x, axis=-1, keepdims=True)
            return (x - mu) * jax.lax.rsqrt(var + LN_EPS) * scale + bias
        key = jax.random.key(seed)
        ks = jax.random.split(key, 8)
        B, T, D, E = (4, 2048, 512, 1024)
        s = 0.02
        return {'x': jax.random.normal(ks[0], (B, T, D), jnp.float32), 'emb': jax.random.normal(ks[1], (B, E), jnp.float32), 'src_mask': jax.random.randint(ks[2], (B, T), 0, 2).astype(jnp.int32), 'norm_scale': jnp.ones((D,), jnp.float32), 'norm_bias': jnp.zeros((D,), jnp.float32), 'Wq': jax.random.normal(ks[3], (D, D), jnp.float32) * s, 'bq': jnp.zeros((D,), jnp.float32), 'Wk': jax.random.normal(ks[4], (D, D), jnp.float32) * s, 'bk': jnp.zeros((D,), jnp.float32), 'Wv': jax.random.normal(ks[5], (D, D), jnp.float32) * s, 'bv': jnp.zeros((D,), jnp.float32), 'film_emb_W': jax.random.normal(ks[6], (E, 2 * D), jnp.float32) * s, 'film_emb_b': jnp.zeros((2 * D,), jnp.float32), 'film_norm_scale': jnp.ones((D,), jnp.float32), 'film_norm_bias': jnp.zeros((D,), jnp.float32), 'film_out_W': jax.random.normal(ks[7], (D, D), jnp.float32) * s, 'film_out_b': jnp.zeros((D,), jnp.float32)}
    _L0_cond_all = _L0_cond_setup()
    _L0_cond_in = {k: v for k, v in _L0_cond_all.items() if k in ('norm_scale', 'norm_bias', 'Wq', 'bq', 'Wk', 'bk', 'Wv', 'bv', 'film_emb_W', 'film_emb_b', 'film_norm_scale', 'film_norm_bias', 'film_out_W', 'film_out_b')}
    del _L0_cond_all

    def _L1_cond_setup():
        import jax, jax.numpy as jnp
        import numpy as np
        B, T, D, H, TE = (4, 1024, 512, 8, 1024)
        EPS = 1e-05

        def _ln(x, w, b):
            m = jnp.mean(x, axis=-1, keepdims=True)
            v = jnp.mean((x - m) ** 2, axis=-1, keepdims=True)
            return (x - m) * jax.lax.rsqrt(v + EPS) * w + b
        key = jax.random.key(seed)
        ks = jax.random.split(key, 16)
        s = 0.02
        inp = {'x': jax.random.normal(ks[0], (B, T, D), jnp.float32), 'emb': jax.random.normal(ks[1], (B, TE), jnp.float32), 'src_mask': (jax.random.uniform(ks[2], (B, T, 1)) > 0.2).astype(jnp.float32), 'num_head': H, 'ln_w': jnp.ones((D,), jnp.float32), 'ln_b': jnp.zeros((D,), jnp.float32), 'Wq': jax.random.normal(ks[3], (D, D), jnp.float32) * s, 'bq': jnp.zeros((D,), jnp.float32), 'Wk': jax.random.normal(ks[4], (D, D), jnp.float32) * s, 'bk': jnp.zeros((D,), jnp.float32), 'Wv': jax.random.normal(ks[5], (D, D), jnp.float32) * s, 'bv': jnp.zeros((D,), jnp.float32), 'W_emb': jax.random.normal(ks[6], (TE, 2 * D), jnp.float32) * s, 'b_emb': jnp.zeros((2 * D,), jnp.float32), 'ln2_w': jnp.ones((D,), jnp.float32), 'ln2_b': jnp.zeros((D,), jnp.float32), 'W_out': jax.random.normal(ks[7], (D, D), jnp.float32) * s, 'b_out': jnp.zeros((D,), jnp.float32)}
        return inp
    _L1_cond_all = _L1_cond_setup()
    _L1_cond_in = {k: v for k, v in _L1_cond_all.items() if k in ('ln_w', 'ln_b', 'Wq', 'bq', 'Wk', 'bk', 'Wv', 'bv', 'W_emb', 'b_emb', 'ln2_w', 'ln2_b', 'W_out', 'b_out')}
    del _L1_cond_all
    return {'x': x, 'cond_2048': cond_2048, 'mask_BxS_ik0': mask_BxS_ik0, 'mask_BxSx1_fk1': mask_BxSx1_fk1, 'L0_cond_norm_scale': _L0_cond_in['norm_scale'], 'L0_cond_norm_bias': _L0_cond_in['norm_bias'], 'L0_cond_Wq': _L0_cond_in['Wq'], 'L0_cond_bq': _L0_cond_in['bq'], 'L0_cond_Wk': _L0_cond_in['Wk'], 'L0_cond_bk': _L0_cond_in['bk'], 'L0_cond_Wv': _L0_cond_in['Wv'], 'L0_cond_bv': _L0_cond_in['bv'], 'L0_cond_film_emb_W': _L0_cond_in['film_emb_W'], 'L0_cond_film_emb_b': _L0_cond_in['film_emb_b'], 'L0_cond_film_norm_scale': _L0_cond_in['film_norm_scale'], 'L0_cond_film_norm_bias': _L0_cond_in['film_norm_bias'], 'L0_cond_film_out_W': _L0_cond_in['film_out_W'], 'L0_cond_film_out_b': _L0_cond_in['film_out_b'], 'L1_cond_ln_w': _L1_cond_in['ln_w'], 'L1_cond_ln_b': _L1_cond_in['ln_b'], 'L1_cond_Wq': _L1_cond_in['Wq'], 'L1_cond_bq': _L1_cond_in['bq'], 'L1_cond_Wk': _L1_cond_in['Wk'], 'L1_cond_bk': _L1_cond_in['bk'], 'L1_cond_Wv': _L1_cond_in['Wv'], 'L1_cond_bv': _L1_cond_in['bv'], 'L1_cond_W_emb': _L1_cond_in['W_emb'], 'L1_cond_b_emb': _L1_cond_in['b_emb'], 'L1_cond_ln2_w': _L1_cond_in['ln2_w'], 'L1_cond_ln2_b': _L1_cond_in['ln2_b'], 'L1_cond_W_out': _L1_cond_in['W_out'], 'L1_cond_b_out': _L1_cond_in['b_out']}

def reference(x, cond_2048, mask_BxS_ik0, mask_BxSx1_fk1, L0_cond_norm_scale, L0_cond_norm_bias, L0_cond_Wq, L0_cond_bq, L0_cond_Wk, L0_cond_bk, L0_cond_Wv, L0_cond_bv, L0_cond_film_emb_W, L0_cond_film_emb_b, L0_cond_film_norm_scale, L0_cond_film_norm_bias, L0_cond_film_out_W, L0_cond_film_out_b, L1_cond_ln_w, L1_cond_ln_b, L1_cond_Wq, L1_cond_bq, L1_cond_Wk, L1_cond_bk, L1_cond_Wv, L1_cond_bv, L1_cond_W_emb, L1_cond_b_emb, L1_cond_ln2_w, L1_cond_ln2_b, L1_cond_W_out, L1_cond_b_out):
    import jax
    import jax.numpy as jnp

    def _L0_cond_ref(x, emb, src_mask, norm_scale, norm_bias, Wq, bq, Wk, bk, Wv, bv, film_emb_W, film_emb_b, film_norm_scale, film_norm_bias, film_out_W, film_out_b):
        import jax, jax.numpy as jnp
        import numpy as np
        H = 16
        LN_EPS = 1e-05

        def _layernorm(x, scale, bias):
            mu = jnp.mean(x, axis=-1, keepdims=True)
            var = jnp.var(x, axis=-1, keepdims=True)
            return (x - mu) * jax.lax.rsqrt(var + LN_EPS) * scale + bias
        B, T, D = x.shape
        dh = D // H
        xn = _layernorm(x, norm_scale, norm_bias)
        q = xn @ Wq + bq
        k = xn @ Wk + bk
        v = xn @ Wv + bv
        mask = (src_mask == 1)[:, :, None]
        k = jnp.where(mask, -jnp.inf, k)
        v = jnp.where(mask, 0.0, v)
        q = q.reshape(B, T, H, dh).transpose(0, 2, 1, 3)
        k = k.reshape(B, T, H, dh).transpose(0, 2, 1, 3)
        v = v.reshape(B, T, H, dh).transpose(0, 2, 1, 3)
        q = jax.nn.softmax(q, axis=-1)
        k = jax.nn.softmax(k, axis=2)
        attn = jnp.einsum('bhse,bhsd->bhed', k, v)
        y = jnp.einsum('bhtd,bhed->bhte', q, attn)
        y = y.transpose(0, 2, 1, 3).reshape(B, T, D)
        emb_out = jax.nn.silu(emb) @ film_emb_W + film_emb_b
        scale, shift = jnp.split(emb_out, 2, axis=-1)
        h = _layernorm(y, film_norm_scale, film_norm_bias) * (1.0 + scale[:, None, :]) + shift[:, None, :]
        h = jax.nn.silu(h) @ film_out_W + film_out_b
        return x + h

    def _L1_cond_ref(x, emb, src_mask, num_head, ln_w, ln_b, Wq, bq, Wk, bk, Wv, bv, W_emb, b_emb, ln2_w, ln2_b, W_out, b_out):
        import jax, jax.numpy as jnp
        import numpy as np
        B, T, D, H, TE = (4, 1024, 512, 8, 1024)
        EPS = 1e-05

        def _ln(x, w, b):
            m = jnp.mean(x, axis=-1, keepdims=True)
            v = jnp.mean((x - m) ** 2, axis=-1, keepdims=True)
            return (x - m) * jax.lax.rsqrt(v + EPS) * w + b
        b, t, d = x.shape
        h = num_head
        dh = d // h
        xn = _ln(x, ln_w, ln_b)
        q = xn @ Wq + bq
        k = xn @ Wk + bk + (1.0 - src_mask) * -1000000.0
        q = jax.nn.softmax(q.reshape(b, t, h, dh), axis=-1)
        k = jax.nn.softmax(k.reshape(b, t, h, dh), axis=1)
        v = ((xn @ Wv + bv) * src_mask).reshape(b, t, h, dh)
        att = jnp.einsum('bnhd,bnhl->bhdl', k, v)
        y = jnp.einsum('bnhd,bhdl->bnhl', q, att).reshape(b, t, d)
        emb_out = (jax.nn.silu(emb) @ W_emb + b_emb)[:, None, :]
        scale, shift = jnp.split(emb_out, 2, axis=2)
        hh = _ln(y, ln2_w, ln2_b) * (1.0 + scale) + shift
        hh = jax.nn.silu(hh) @ W_out + b_out
        return x + hh
    x = _L0_cond_ref(x, cond_2048, mask_BxS_ik0, L0_cond_norm_scale, L0_cond_norm_bias, L0_cond_Wq, L0_cond_bq, L0_cond_Wk, L0_cond_bk, L0_cond_Wv, L0_cond_bv, L0_cond_film_emb_W, L0_cond_film_emb_b, L0_cond_film_norm_scale, L0_cond_film_norm_bias, L0_cond_film_out_W, L0_cond_film_out_b)
    x = _L1_cond_ref(x, cond_2048, mask_BxSx1_fk1, 8, L1_cond_ln_w, L1_cond_ln_b, L1_cond_Wq, L1_cond_bq, L1_cond_Wk, L1_cond_bk, L1_cond_Wv, L1_cond_bv, L1_cond_W_emb, L1_cond_b_emb, L1_cond_ln2_w, L1_cond_ln2_b, L1_cond_W_out, L1_cond_b_out)
    return x

_drawn_inputs = setup_inputs


def setup_inputs(seed=0):
    import zlib

    import numpy as np

    out = dict(_drawn_inputs(seed))
    spreads = {'L0_cond_norm_scale': (1.0, 0.2),
     'L0_cond_norm_bias': (0.0, 0.1),
     'L0_cond_bq': (0.0, 0.285),
     'L0_cond_bk': (0.0, 0.8),
     'L0_cond_bv': (0.0, 0.1),
     'L0_cond_film_emb_b': (0.0, 0.1),
     'L0_cond_film_norm_scale': (1.0, 0.2),
     'L0_cond_film_norm_bias': (0.0, 0.289),
     'L0_cond_film_out_b': (0.0, 0.1),
     'L1_cond_ln_w': (1.0, 0.2),
     'L1_cond_ln_b': (0.0, 0.273),
     'L1_cond_bq': (0.0, 0.8),
     'L1_cond_bk': (0.0, 0.1),
     'L1_cond_bv': (0.0, 0.1),
     'L1_cond_b_emb': (0.0, 0.1),
     'L1_cond_ln2_w': (1.0, 0.2),
     'L1_cond_ln2_b': (0.0, 0.285),
     'L1_cond_b_out': (0.0, 0.1)}
    factors = {'L1_cond_Wq': 8.0}
    for name, (base, spread) in spreads.items():
        noise = np.random.default_rng([zlib.crc32(name.encode()), seed]).standard_normal(out[name].shape)
        drawn = base * np.exp(spread * noise) if base else spread * noise
        out[name] = jnp.asarray(drawn.astype(out[name].dtype))
    for name, factor in factors.items():
        out[name] = (out[name] * factor).astype(out[name].dtype)
    return out
```

```python
from contextlib import ExitStack

import concourse.bass as bass
from concourse import mybir

F32 = mybir.dt.float32
F32R = mybir.dt.float32r
I32 = mybir.dt.int32
ALU = mybir.AluOpType
ACT = mybir.ActivationFunctionType
AX = mybir.AxisListType

P = 128
VECTORS = ["norm_scale", "norm_bias", "bk", "film_scale", "film_bias", "film_b"]
MATS = ["k", "v", "q", "o"]
EPS = 1e-5
BIG = 2.0 ** 127
HUGE = 3.0e38


def build_blocks(nc, x, cond, mask0, mask1, weights, film_w, vec_rows, bias_rows, out):
    B, T, D = x.shape
    E = cond.shape[1]
    C = D // P
    EC = E // P
    NT = 2 * B
    PAIR = 2 * T
    Q = P // 32
    HEAD = [D // 16, D // 8]
    NSTEP = NT
    VROWS = vec_rows.shape[0] // 2
    assert T == P and C == 4 and E == 2 * D

    row_of, at = {}, 0
    for name in VECTORS:
        row_of[name] = at
        at += (2 * D if name == "film_b" else D) // P
    assert at == VROWS

    ctx = ExitStack()
    with ctx:
        def sb(name, shape, dt=F32):
            return ctx.enter_context(nc.sbuf_tensor(name, shape, dt))

        def sem(name):
            return ctx.enter_context(nc.semaphore(name))

        X = sb("X", [P, B, D])
        WH = [sb(f"WH_{m}", [P, C, D], F32R) for m in MATS]
        WL = [sb(f"WL_{m}", [P, C, D], F32R) for m in MATS]
        STAGE = sb("STAGE", [P, 2, C, D])
        XN = sb("XN", [P, 2, 2 * P])
        XF = sb("XF", [P, 2, PAIR])
        XH = [sb(f"XH{n}", [P, C, PAIR], F32R) for n in range(2)]
        XL = [sb(f"XL{n}", [P, C, PAIR], F32R) for n in range(2)]
        SK = [sb(f"SK{n}", [P, C, PAIR]) for n in range(2)]
        SQ = [sb(f"SQ{n}", [P, D]) for n in range(2)]
        VV = sb("VV", [P, 3, C, P + 1])
        EK = sb("EK", [P, D])
        EQ = sb("EQ", [P, D])
        ATT = sb("ATT", [P, 2, 2 * (P + Q)])
        YN = sb("YN", [P, D])
        Z = sb("Z", [P, D])
        H = sb("H", [P, D])
        HH = sb("HH", [P, D], F32R)
        HL = sb("HL", [P, D], F32R)
        BR = sb("BR", [P, D], F32R)
        MK = [sb(f"MK{l}", [P, T], F32R) for l in range(2)]
        SEL = sb("SEL", [P, B], F32R)
        ident = sb("ident", [P, P])
        VALID = [sb(f"VALID{l}", [P, B]) for l in range(2)]
        CT = sb("CT", [P, EC, B])
        G = sb("G", [P, C, B])
        U = sb("U", [P, C, B])
        FA = [sb(f"FA{l}", [P, C, B]) for l in range(2)]
        FC = [sb(f"FC{l}", [P, C, B]) for l in range(2)]
        VC = sb("VC", [P, 2 * VROWS])
        half = sb("half", [P, 1])
        RING = 8
        BNX, BNY = sb("BNX", [P, 6]), sb("BNY", [P, 6])
        MVX = sb("MVX", [P, RING, 2])
        RSX = sb("RSX", [P, RING])
        VEX = sb("VEX", [P, 1])
        MVY = sb("MVY", [P, 2])
        RSY = sb("RSY", [P, 1])
        VEY = sb("VEY", [P, 1])
        KM = sb("KM", [P, 2, 2])
        KB = sb("KB", [P, 2, 2])
        QM = sb("QM", [P, D // min(HEAD)])
        AB = sb("AB", [P, 2, 2, 32])
        RK = sb("RK", [P, 2, 2, 1])
        RQ = sb("RQ", [P, 16])

        ones = EK[:, 0:P]
        VR = H[0:2 * VROWS, 0:P]
        COND = SK[1][0:B, :, :].rearrange("b c n -> b (c n)")
        CTH = [Z[0:B, :], EQ[0:B, :]]
        BIAS = [YN[0:6, :], YN[32:38, :]]
        BTMP = SQ[0][32:38, :]
        MI = SQ[1][0:B, 0:T].bitcast(I32)
        MF = SQ[1][0:2 * B, T:2 * T]
        MT = SQ[1][0:2 * B, 2 * T:3 * T]
        MTMP = SQ[1][B:2 * B, 3 * T:4 * T]
        FIRST_STAGE = [STAGE[:, 0], STAGE[:, 1], X[:, 8:12, :], X[:, 12:16, :]]
        FILM0 = X[:, 16:32, :].rearrange("p (k h) n -> p k h n", h=2)
        film_stage = STAGE[:, :, :, :].rearrange("p a c n -> p (a c) n")

        PS = ctx.enter_context(nc.psum_tensor("PS", [P, 8, 512], F32))
        B_K, B_VO, B_Q, B_XK, B_TQ, B_TY, B_ATT = 0, 1, 2, 3, 4, 5, 6

        XLOADS = [(0, 1), (1, 1), (2, 2), (4, 4), (8, 4), (12, 4), (16, 8), (24, 8)]
        ld_x = [sem(f"ld_x{n}") for n in range(len(XLOADS))]
        ld_w = [sem(f"ld_w{n}") for n in range(8)]
        ld_film = [sem(f"ld_film{n}") for n in range(4)]
        ld_vec, ld_bias, ld_mask, ld_cond = sem("ld_vec"), sem("ld_bias"), sem("ld_mask"), sem("ld_cond")
        st_out = sem("st_out")
        pool_const, pool_x, pool_y = sem("pool_const"), sem("pool_x"), sem("pool_y")
        pool_own = sem("pool_own")
        pe_vec, pe_cond, pe_valid, pe_count = sem("pe_vec"), sem("pe_cond"), sem("pe_valid"), sem("pe_count")
        pe_k, pe_v, pe_q, pe_o = sem("pe_k"), sem("pe_v"), sem("pe_q"), sem("pe_o")
        pe_tk, pe_tq, pe_ty, pe_a = sem("pe_tk"), sem("pe_tq"), sem("pe_ty"), sem("pe_a")
        pe_att, pe_y, pe_film = sem("pe_att"), sem("pe_y"), sem("pe_film")
        act_cond, act_w = sem("act_cond"), sem("act_w")
        act_ek, act_eq, act_z, act_t = sem("act_ek"), sem("act_eq"), sem("act_z"), sem("act_t")
        act_v, act_hh, act_xf, act_xh = sem("act_v"), sem("act_hh"), sem("act_xf"), sem("act_xh")
        dve_vec, dve_const, dve_cond, dve_mask = sem("dve_vec"), sem("dve_const"), sem("dve_cond"), sem("dve_mask")
        dve_w, dve_ks, dve_qs, dve_stat = sem("dve_w"), sem("dve_ks"), sem("dve_qs"), sem("dve_stat")
        dve_xn, dve_xl, dve_x = sem("dve_xn"), sem("dve_xl"), sem("dve_x")
        dve_att, dve_yr, dve_ystat, dve_yn = sem("dve_att"), sem("dve_yr"), sem("dve_ystat"), sem("dve_yn")
        dve_mask_rows, dve_valid = sem("dve_mask_rows"), sem("dve_valid")
        dve_h, dve_hl, dve_film, dve_own = sem("dve_h"), sem("dve_hl"), sem("dve_film"), sem("dve_own")

        def vec(l, name, c0=0, n=C):
            r = l * VROWS + row_of[name] + c0
            return VC[:, r:r + n]

        def x_load_of(tile):
            return next(n for n, (a, k) in enumerate(XLOADS) if a <= tile < a + k)

        def film_at(s):
            return {0: 0, 1: 1, 6: 2, 10: 3}.get(s)

        def stats_at(s):
            return {-2: [0, 1], -1: [2, 3]}.get(s, [s + 4] if s + 4 < NT else [])

        SPLIT_AT = {"mid": {31: [4]}, "end": {31: [5], 34: [7]}, "start": {32: [6]}}
        LAST_USE = {4: pe_k, 5: pe_v, 6: pe_q, 7: pe_o}
        SLOTS = range(-2, NT + 3)

        block = ctx.enter_context(nc.Block())

        @block.sync
        def _(eng):
            def load_x(n):
                a, k = XLOADS[n]
                eng.dma_start(X[:, a:a + k, :], x[a:a + k].rearrange("b t d -> t b d")).then_inc(ld_x[n], 16)

            def load_w(w):
                dst = FIRST_STAGE[w] if w < 4 else STAGE[:, w % 2]
                src = weights[w // 4][w % 4].rearrange("(c p) n -> p c n", p=P)
                eng.dma_start(dst, src).then_inc(ld_w[w], 16)

            load_x(0)
            load_x(1)
            load_w(0)
            load_w(1)
            load_w(2)
            load_x(2)
            eng.dma_start(FILM0, film_w[0].rearrange("(k p) (h n) -> p k h n", p=P, h=2)).then_inc(ld_film[0], 16)
            load_w(3)
            load_x(3)
            eng.wait_ge(dve_w, 3 * C)
            load_x(4)
            eng.wait_ge(dve_w, 4 * C)
            load_x(5)
            film1 = film_w[1].rearrange("(k p) (h n) -> p k h n", p=P, h=2)
            eng.dma_start(film_stage, film1[:, :, 0, :]).then_inc(ld_film[2], 16)
            eng.wait_ge(pe_film, 2)
            load_x(6)
            load_x(7)
            eng.wait_ge(pe_film, 3)
            eng.dma_start(film_stage, film1[:, :, 1, :]).then_inc(ld_film[3], 16)
            eng.wait_ge(pe_film, 4)
            load_w(4)
            load_w(5)
            eng.wait_ge(dve_w, 5 * C)
            load_w(6)
            eng.wait_ge(dve_w, 6 * C)
            load_w(7)
            for b in range(B):
                eng.wait_ge(dve_x, B + b + 1)
                eng.dma_start(out[b], X[:, b, :]).then_inc(st_out, 16)
            eng.wait_ge(st_out, 16 * B)

        @block.gpsimd
        def _(eng):
            eng.memset(ident[:, :], 0.0).then_inc(pool_own, 1)
            eng.wait_ge(pool_own, 1)
            eng.affine_select(out=ident[:, :], in_=ident[:, :], compare_op=ALU.not_equal, fill=1.0,
                              base=0, pattern=[[-1, P]], channel_multiplier=1).then_inc(pool_const, 1)
            eng.memset(half[:, :], -0.5).then_inc(pool_const, 1)
            eng.memset(ones, 1.0).then_inc(pool_const, 1)
            eng.memset(ATT[:, :, :], 0.0).then_inc(pool_const, 1)
            eng.memset(VV[:, :, :, P:P + 1], 1.0).then_inc(pool_const, 1)
            eng.wait_ge(pool_const, 2)
            own = [1]

            def root(var, plus, out_):
                eng.tensor_scalar(plus, var, EPS, None, ALU.add).then_inc(pool_own, 1)
                own[0] += 1
                eng.wait_ge(pool_own, own[0])
                return eng.tensor_tensor(out_, plus, half[:, :], ALU.pow)

            def root_x(n):
                eng.wait_ge(dve_stat, n + 1)
                root(MVX[:, n % RING, 1:2], VEX[:, :], RSX[:, n % RING:n % RING + 1]).then_inc(pool_x, 1)
                eng.wait_ge(pool_x, n + 1)

            def root_y(j):
                eng.wait_ge(dve_ystat, j + 1)
                root(MVY[:, 1:2], VEY[:, :], RSY[:, :]).then_inc(pool_y, 1)
                eng.wait_ge(pool_y, j + 1)

            for s in SLOTS:
                for n in stats_at(s):
                    root_x(n)
                if 0 <= s - 2 < NT:
                    root_y(s - 2)

        @block.scalar
        def _(eng):
            eng.dma_start(VR, vec_rows).then_inc(ld_vec, 16)
            eng.dma_start(COND, cond).then_inc(ld_cond, 16)
            eng.dma_start(MI, mask0).then_inc(ld_mask, 16)
            for n in range(2):
                eng.dma_start(MF[B * n:B * n + B, :], mask1).then_inc(ld_mask, 16)
                eng.dma_start(BIAS[n], bias_rows).then_inc(ld_bias, 16)
            eng.wait_ge(ld_cond, 16)
            for n in range(2):
                eng.activation(CTH[n], COND[:, n * D:n * D + D], ACT.Tanh, scale=0.5).then_inc(act_cond, 1)

            def split_high(w):
                eng.wait_ge(ld_w[w], 16)
                if w in LAST_USE:
                    eng.wait_ge(LAST_USE[w], B)
                src = FIRST_STAGE[w] if w < 4 else STAGE[:, w % 2]
                for c in range(C):
                    eng.activation(WH[w % 4][:, c, :], src[:, c, :], ACT.Copy).then_inc(act_w, 1)

            def exp_k(j):
                eng.wait_ge(pe_tk, j + 1)
                eng.wait_ge(pe_att, j)
                eng.activation(EK[:, :], PS[:, B_XK, :], ACT.Exp).then_inc(act_ek, 1)

            def exp_q(j):
                eng.wait_ge(pe_tq, j + 1)
                eng.wait_ge(pe_y, j)
                eng.activation(EQ[:, :], PS[:, B_TQ, :], ACT.Exp).then_inc(act_eq, 1)

            def film(o):
                l, b = divmod(o, B)
                eng.wait_ge(pe_ty, o + 1)
                eng.wait_ge(dve_film, 2 * (l + 1))
                eng.wait_ge(dve_h, o)
                for c in range(C):
                    z = eng.activation(Z[:, c * P:c * P + P], PS[:, B_TY, c * P:c * P + P], ACT.Identity,
                                       bias=FC[l][:, c, b:b + 1], scale=FA[l][:, c, b:b + 1])
                z.then_inc(act_z, 1)
                eng.wait_ge(act_z, o + 1)
                eng.wait_ge(dve_hl, o)
                eng.activation(H[:, :], Z[:, :], ACT.Tanh).then_inc(act_t, 1)

            def values(i):
                l, b = divmod(i, B)
                eng.wait_ge(pe_v, i + 1)
                if i >= 3:
                    eng.wait_ge(pe_att, i - 2)
                eng.wait_ge(dve_mask, 1)
                eng.activation(VV[:, i % 3, :, 0:P], PS[:, B_VO, :].rearrange("p (c n) -> p c n", c=C),
                               ACT.Copy, scale=VALID[l][:, b:b + 1]).then_inc(act_v, 1)

            def h_high(o):
                eng.wait_ge(dve_h, o + 1)
                eng.wait_ge(pe_o, o)
                eng.activation(HH[:, :], H[:, :], ACT.Copy).then_inc(act_hh, 1)

            def x_turned(m):
                g, p = divmod(m, 2)
                l = g // (B // 2)
                eng.wait_ge(pe_a, m + 1)
                if m == 0:
                    eng.wait_ge(dve_vec, 1)
                eng.wait_ge(dve_xl, m)
                eng.wait_ge(act_xh, m)
                for cc in range(2):
                    f = eng.activation(XF[:, cc, :], PS[:, B_XK, cc * PAIR:(cc + 1) * PAIR], ACT.Identity,
                                       bias=vec(l, "norm_bias", 2 * p + cc, 1),
                                       scale=vec(l, "norm_scale", 2 * p + cc, 1))
                f.then_inc(act_xf, 1)
                eng.wait_ge(act_xf, m + 1)
                if g >= 2:
                    eng.wait_ge(pe_q, 2 * g - 2)
                eng.activation(XH[g % 2][:, 2 * p:2 * p + 2, :], XF[:, :, :], ACT.Copy).then_inc(act_xh, 1)

            for s in SLOTS:
                i, j, o, m = s, s - 2, s - 3, s + 2
                for w in SPLIT_AT["start"].get(s, []):
                    split_high(w)
                if 0 <= j < NT:
                    exp_k(j)
                    exp_q(j)
                if 0 <= o < NT:
                    film(o)
                for w in SPLIT_AT["mid"].get(s, []):
                    split_high(w)
                if 0 <= i < NT:
                    values(i)
                if 0 <= o < NT:
                    h_high(o)
                if m < NSTEP:
                    x_turned(m)
                if s == -1:
                    for w in range(3):
                        split_high(w)
                if s == 0:
                    split_high(3)
                for w in SPLIT_AT["end"].get(s, []):
                    split_high(w)

        @block.tensor
        def _(eng):
            def bank(b, a=0, n=512):
                return PS[:, b, a:a + n]

            def weights_ready(w):
                eng.wait_ge(act_w, C * (w + 1))
                eng.wait_ge(dve_w, C * (w + 1))

            def split_product(dst, left, right, first=True, last=True):
                for c in range(C):
                    for a, b in ((0, 0), (0, 1), (1, 0)):
                        mm = eng.matmul(dst, left[a](c), right[b](c), start=(first and c == 0 and a + b == 0),
                                        stop=(last and c == C - 1 and a == 1))
                return mm

            def picked(r):
                return SEL[:, r:r + 1].to_broadcast([P, P])

            def keys(i):
                g, p = divmod(i, 2)
                l = i // B
                eng.wait_ge(act_xh, 2 * g + 2)
                eng.wait_ge(dve_xl, 2 * g + 2)
                eng.wait_ge(dve_ks, i)
                weights_ready(4 * l)
                if i == 0:
                    eng.wait_ge(dve_mask, 1)
                xs = [lambda c: XH[g % 2][:, c, :], lambda c: XL[g % 2][:, c, :]]
                for cc in range(2):
                    f = (2 * p + cc) * P
                    ws = [lambda c: WH[0][:, c, f:f + P], lambda c: WL[0][:, c, f:f + P]]
                    split_product(bank(B_K, cc * PAIR, PAIR), ws, xs, last=False)
                    for t in range(2):
                        b = (2 * g + t) % B
                        mm = eng.matmul(bank(B_K, cc * PAIR + t * T, T), picked(b), MK[l][:, :],
                                        start=False, stop=(t == 1))
                mm.then_inc(pe_k, 1)

            def project_x(i, mat, dst, done):
                l, g, t = i // B, i // 2, i % 2
                xs = [lambda c: XH[g % 2][:, c, t * T:t * T + T], lambda c: XL[g % 2][:, c, t * T:t * T + T]]
                ws = [lambda c: WH[mat][:, c, :], lambda c: WL[mat][:, c, :]]
                weights_ready(4 * l + mat)
                split_product(dst, xs, ws, last=False)
                eng.matmul(dst, picked(3 * l + mat - 1), BR[:, :], start=False, stop=True).then_inc(done, 1)

            def values(i):
                if i:
                    eng.wait_ge(act_v, i)
                if i >= 4:
                    eng.wait_ge(dve_x, i - 3)
                project_x(i, 1, bank(B_VO), pe_v)

            def queries(i):
                eng.wait_ge(dve_qs, i)
                done = sum(1 for s in range(i) if film_at(s) is not None)
                eng.wait_ge(dve_film, done)
                project_x(i, 2, bank(B_Q), pe_q)

            def turn_keys(j):
                g, t = divmod(j, 2)
                eng.wait_ge(dve_ks, 2 * g + 2)
                eng.wait_ge(act_xf, min(j + 4, NSTEP))
                for c in range(C):
                    mm = eng.transpose(bank(B_XK, c * P, P), SK[g % 2][:, c, t * T:t * T + T], ident[:, :])
                mm.then_inc(pe_tk, 1)

            def turn_queries(j):
                eng.wait_ge(dve_qs, j + 1)
                eng.wait_ge(act_eq, j)
                for c in range(C):
                    mm = eng.transpose(bank(B_TQ, c * P, P), SQ[j % 2][:, c * P:c * P + P], ident[:, :])
                mm.then_inc(pe_tq, 1)

            def turn_y(o):
                eng.wait_ge(dve_yn, o + 1)
                eng.wait_ge(act_z, o)
                for c in range(C):
                    mm = eng.transpose(bank(B_TY, c * P, P), YN[:, c * P:c * P + P], ident[:, :])
                mm.then_inc(pe_ty, 1)

            def attention(j):
                eng.wait_ge(act_ek, j + 1)
                eng.wait_ge(act_v, j + 1)
                eng.wait_ge(dve_yr, j)
                for c in range(C):
                    mm = eng.matmul(bank(B_ATT + c // 2, (c % 2) * (P + 1), P + 1), EK[:, c * P:c * P + P],
                                    VV[:, j % 3, c, :], start=True, stop=True)
                mm.then_inc(pe_att, 1)

            def mix(j):
                eng.wait_ge(act_eq, j + 1)
                eng.wait_ge(dve_att, j + 1)
                W = P + Q
                for c in range(C):
                    mm = eng.matmul(bank(B_ATT + c // 2, (c % 2) * W, W), EQ[:, c * P:c * P + P],
                                    ATT[:, c // 2, (c % 2) * W:(c % 2 + 1) * W], start=True, stop=True)
                mm.then_inc(pe_y, 1)

            def output(o):
                l = o // B
                eng.wait_ge(act_hh, o + 1)
                eng.wait_ge(dve_hl, o + 1)
                eng.wait_ge(act_v, min(o + 4, NT))
                weights_ready(4 * l + 3)
                hs = [lambda c: HH[:, c * P:c * P + P], lambda c: HL[:, c * P:c * P + P]]
                ws = [lambda c: WH[3][:, c, :], lambda c: WL[3][:, c, :]]
                split_product(bank(B_VO), hs, ws, last=False)
                eng.matmul(bank(B_VO), picked(3 * l + 2), BR[:, :], start=False, stop=True).then_inc(pe_o, 1)

            def turn_x(m):
                eng.wait_ge(dve_xn, m + 1)
                eng.wait_ge(act_xf, m)
                if m >= 4:
                    eng.wait_ge(act_ek, m - 3)
                for cc in range(2):
                    for t in range(2):
                        mm = eng.transpose(bank(B_XK, cc * PAIR + t * T, T), XN[:, t, cc * P:cc * P + P], ident[:, :])
                mm.then_inc(pe_a, 1)

            def conditioning(n):
                eng.wait_ge(ld_film[n & 2 if n < 2 else n], 16)
                eng.wait_ge(dve_cond, 2)
                w = FILM0[:, :, n, :] if n < 2 else film_stage
                for c in range(C):
                    for k in range(EC):
                        mm = eng.matmul(bank(B_Q, c * B, B), w[:, k, c * P:c * P + P], CT[:, k, :],
                                        start=(k == 0), stop=(k == EC - 1))
                mm.then_inc(pe_film, 1)

            eng.wait_ge(pool_const, 5)
            eng.wait_ge(ld_vec, 16)
            n = 2 * VROWS
            eng.transpose(bank(B_TY, 0, n), VR, ident[0:n, 0:n]).then_inc(pe_vec, 1)
            for s in SLOTS:
                i, j, o, m = s, s - 2, s - 3, s + 2
                if s == 0:
                    eng.wait_ge(dve_mask_rows, 1)
                    for l in range(2):
                        mm = eng.transpose(bank(B_Q, l * B, B), MT[0:B, :] if l == 0 else MF[0:B, :], ident[0:B, 0:B])
                    mm.then_inc(pe_valid, 1)
                    eng.wait_ge(dve_valid, 1)
                    eng.matmul(bank(B_TQ, 0, B), ones, VALID[0][:, :], start=True, stop=True).then_inc(pe_count, 1)
                    eng.wait_ge(dve_cond, 1)
                    for k in range(EC):
                        mm = eng.transpose(bank(B_TY, k * B, B), COND[:, k * P:k * P + P], ident[0:B, 0:B])
                    mm.then_inc(pe_cond, 1)
                if 0 <= i < NT:
                    keys(i)
                if 0 <= j < NT:
                    turn_keys(j)
                    turn_queries(j)
                if 0 <= o < NT:
                    turn_y(o)
                if 0 <= i < NT:
                    values(i)
                if 0 <= j < NT:
                    attention(j)
                if 0 <= i < NT:
                    queries(i)
                if 0 <= j < NT:
                    mix(j)
                if 0 <= o < NT:
                    output(o)
                if m < NSTEP:
                    turn_x(m)
                if film_at(s) is not None:
                    eng.wait_ge(dve_qs, s + 1)
                    conditioning(film_at(s))

        @block.vector
        def _(eng):
            own = [0]

            def then(ins):
                own[0] += 1
                ins.then_inc(dve_own, 1)
                eng.wait_ge(dve_own, own[0])

            def split_low(w):
                src = FIRST_STAGE[w] if w < 4 else STAGE[:, w % 2]
                eng.wait_ge(ld_w[w], 16)
                for c in range(C):
                    eng.wait_ge(act_w, C * w + c + 1)
                    eng.tensor_tensor(WL[w % 4][:, c, :], src[:, c, :], WH[w % 4][:, c, :].bitcast(F32),
                                      ALU.subtract).then_inc(dve_w, 1)

            def stat_x(n):
                if n < B:
                    if n in [a for a, _ in XLOADS]:
                        eng.wait_ge(ld_x[x_load_of(n)], 16)
                else:
                    eng.wait_ge(dve_x, n - B + 1)
                then(eng.bn_stats(BNX[:, :], X[:, n % B, :]))
                if n >= RING:
                    eng.wait_ge(pool_x, n - RING + 1)
                eng.bn_aggr(MVX[:, n % RING, :], BNX[:, :]).then_inc(dve_stat, 1)
                eng.wait_ge(dve_stat, n + 1)

            def norm_x(m):
                g, p = divmod(m, 2)
                eng.wait_ge(pool_x, 2 * g + 2)
                eng.wait_ge(pe_a, m)
                for t in range(2):
                    n = 2 * g + t
                    r = n % RING
                    ins = eng.tensor_scalar(XN[:, t, :], X[:, n % B, 2 * p * P:2 * (p + 1) * P], MVX[:, r, 0:1],
                                            RSX[:, r:r + 1], ALU.subtract, ALU.mult)
                ins.then_inc(dve_xn, 1)

            def x_low(m):
                g, p = divmod(m, 2)
                eng.wait_ge(act_xh, m + 1)
                if g >= 2:
                    eng.wait_ge(pe_q, 2 * g - 2)
                dst = slice(2 * p, 2 * p + 2)
                eng.tensor_tensor(XL[g % 2][:, dst, :], XF[:, :, :], XH[g % 2][:, dst, :].bitcast(F32),
                                  ALU.subtract).then_inc(dve_xl, 1)

            def keys(i):
                l, g, p = i // B, i // 2, i % 2
                eng.wait_ge(pe_k, i + 1)
                ps = PS[:, B_K, :].rearrange("p (c t n) -> p c t n", c=2, t=2)
                then(eng.tensor_reduce(KM[:, :, :].rearrange("p c t -> p (c t)"),
                                       PS[:, B_K, :].rearrange("p (a n) -> p a n", n=T), AX.X, ALU.max))
                bk = vec(l, "bk", 2 * p, 2)
                then(eng.tensor_tensor(KB[:, :, :], KM[:, :, :], bk.unsqueeze(2).to_broadcast([P, 2, 2]), ALU.add))
                if g >= 2:
                    eng.wait_ge(pe_tk, 2 * g - 2)
                for cc in range(2):
                    c = 2 * p + cc
                    ins = eng.scalar_tensor_tensor(
                        out=SK[g % 2][:, c, :].rearrange("p (t n) -> p t n", t=2), in0=ps[:, cc],
                        scalar=bk[:, cc:cc + 1], in1=KB[:, cc, :].unsqueeze(2).to_broadcast([P, 2, T]),
                        op0=ALU.add, op1=ALU.subtract)
                ins.then_inc(dve_ks, 1)

            def queries(i):
                w = HEAD[i // B]
                eng.wait_ge(pe_q, i + 1)
                ps = PS[:, B_Q, :].rearrange("p (h n) -> p h n", n=w)
                qm = QM[:, 0:D // w]
                then(eng.tensor_reduce(qm, ps, AX.X, ALU.max))
                if i >= 2:
                    eng.wait_ge(pe_tq, i - 1)
                eng.tensor_tensor(SQ[i % 2][:, :].rearrange("p (h n) -> p h n", n=w), ps,
                                  qm.unsqueeze(2).to_broadcast([P, D // w, w]), ALU.subtract).then_inc(dve_qs, 1)

            def attention(j):
                l = j // B
                w = HEAD[l]
                eng.wait_ge(pe_att, j + 1)
                eng.wait_ge(pe_y, j)
                if j == B:
                    for h in range(P // w):
                        ATT_h = ATT[h * w:(h + 1) * w, :, :]
                        eng.memset(ATT_h[:, :, 2 * h:2 * h + 2], 1.0)
                        eng.memset(ATT_h[:, :, 2 * P + Q + 2 * h:2 * P + Q + 2 * h + 2], 1.0)
                ps = PS[:, B_ATT:B_ATT + 2, 0:2 * (P + 1)].rearrange("p b (c n) -> p b c n", c=2)
                then(eng.reciprocal(RK[:, :, :, :], ps[:, :, :, P:P + 1]))
                dst = ATT[:, :, Q:Q + 2 * P].rearrange("p b (c n) -> p b c n", c=2)
                for h in range(P // w):
                    a, z = h * w, (h + 1) * w
                    to = AB[a:z, :, :, :] if l == 0 else dst[a:z, :, :, a:z]
                    ins = eng.tensor_tensor(to, ps[a:z, :, :, a:z], RK[a:z, :, :, :].to_broadcast([w, 2, 2, w]),
                                            ALU.mult)
                if l == 0:
                    then(ins)
                    for h in range(P // w):
                        a, z = h * w, (h + 1) * w
                        ins = eng.transpose(dst[a:z, :, :, a:z], AB[a:z, :, :, :])
                ins.then_inc(dve_att, 1)

            def mix(j):
                eng.wait_ge(pe_y, j + 1)
                ps = PS[:, B_ATT:B_ATT + 2, 0:Q]
                sums = bass.AP(tensor=ps.tensor, offset=ps.offset, ap=[ps.ap[0], ps.ap[1], [Q + 2 * P, 2], [1, Q]])
                then(eng.reciprocal(RQ[:, :].rearrange("p (b s q) -> p b s q", b=2, s=2), sums))
                eng.wait_ge(pe_ty, j)
                eng.tensor_tensor(YN[:, :].rearrange("p (b h n) -> p b h n", b=2, n=32),
                                  PS[:, B_ATT:B_ATT + 2, Q:Q + 2 * P].rearrange("p b (h n) -> p b h n", n=32),
                                  RQ[:, :].rearrange("p (b h) -> p b h", b=2).unsqueeze(3).to_broadcast([P, 2, 8, 32]),
                                  ALU.mult).then_inc(dve_yr, 1)
                eng.wait_ge(dve_yr, j + 1)
                then(eng.bn_stats(BNY[:, :], YN[:, :]))
                eng.wait_ge(pool_y, j)
                eng.bn_aggr(MVY[:, :], BNY[:, :]).then_inc(dve_ystat, 1)

            def norm_y(j):
                eng.wait_ge(dve_ystat, j + 1)
                eng.wait_ge(pool_y, j + 1)
                eng.tensor_scalar(YN[:, :], YN[:, :], MVY[:, 0:1], RSY[:, :], ALU.subtract, ALU.mult)\
                   .then_inc(dve_yn, 1)

            def h_mul(o):
                eng.wait_ge(act_t, o + 1)
                eng.scalar_tensor_tensor(out=H[:, :], in0=H[:, :], scalar=1.0, in1=Z[:, :],
                                         op0=ALU.add, op1=ALU.mult).then_inc(dve_h, 1)

            def h_low(o):
                eng.wait_ge(act_hh, o + 1)
                eng.wait_ge(dve_h, o + 1)
                eng.wait_ge(pe_o, o)
                eng.tensor_tensor(HL[:, :], H[:, :], HH[:, :].bitcast(F32), ALU.subtract).then_inc(dve_hl, 1)

            def add_x(o):
                eng.wait_ge(pe_o, o + 1)
                b = o % B
                eng.wait_ge(dve_x, o)
                eng.tensor_tensor(X[:, b, :], PS[:, B_VO, :], X[:, b, :], ALU.add).then_inc(dve_x, 1)

            def conditioning(n):
                l, h = divmod(n, 2)
                eng.wait_ge(pe_film, n + 1)
                ps = PS[:, B_Q, 0:C * B].rearrange("p (c b) -> p c b", c=C)

                def wide(v):
                    return v.unsqueeze(2).to_broadcast([P, C, B])

                if h == 0:
                    then(eng.scalar_tensor_tensor(out=G[:, :, :], in0=ps, scalar=1.0, in1=wide(vec(l, "film_b")),
                                                  op0=ALU.add, op1=ALU.add))
                    last = eng.scalar_tensor_tensor(out=FA[l][:, :, :], in0=G[:, :, :], scalar=0.5,
                                                    in1=wide(vec(l, "film_scale")), op0=ALU.mult, op1=ALU.mult)
                else:
                    then(eng.tensor_tensor(U[:, :, :], ps, wide(vec(l, "film_b", C)), ALU.add))
                    then(eng.tensor_tensor(G[:, :, :], G[:, :, :], wide(vec(l, "film_bias")), ALU.mult))
                    then(eng.tensor_tensor(G[:, :, :], G[:, :, :], U[:, :, :], ALU.add))
                    last = eng.tensor_scalar(FC[l][:, :, :], G[:, :, :], 0.5, None, ALU.mult)
                last.then_inc(dve_film, 1)

            def start():
                eng.wait_ge(pool_const, 5)
                for g in range(Q):
                    a, z = 32 * g, 32 * g + 32
                    eng.memset(ATT[a:z, :, g:g + 1], 1.0)
                    eng.memset(ATT[a:z, :, 2 * P + Q + g:2 * P + Q + g + 1], 1.0)
                then(eng.memset(BR[:, :].bitcast(F32), 0.0))
                then(eng.memset(MK[0][:, :].bitcast(F32), 0.0))
                then(eng.memset(MK[1][:, :].bitcast(F32), 0.0))
                then(eng.memset(SEL[:, :].bitcast(F32), 0.0))
                eng.tensor_tensor(SEL[0:2 * B, :], ident[0:2 * B, 0:B], ident[0:2 * B, B:2 * B], ALU.add)
                eng.wait_ge(ld_bias, 32)
                eng.tensor_copy(BR[0:6, :], BIAS[0])
                then(eng.tensor_copy(BTMP.bitcast(F32R), BIAS[1]))
                eng.tensor_tensor(BR[32:38, :], BIAS[1], BTMP, ALU.subtract).then_inc(dve_const, 1)
                eng.wait_ge(ld_mask, 48)
                eng.tensor_scalar(MK[0][0:B, :], MI, 1.0, -BIG, ALU.is_equal, ALU.mult)
                eng.tensor_scalar(MT[0:B, :], MI, 1.0, None, ALU.not_equal).then_inc(dve_mask_rows, 1)

            def start_mask1():
                eng.tensor_scalar(MK[1][0:B, :], MF[0:B, :], 1.0, 1.0e6, ALU.subtract, ALU.mult)
                then(eng.tensor_scalar(MT[B:2 * B, :], MF[B:2 * B, :], 1.0, 1.0e6, ALU.subtract, ALU.mult))
                then(eng.tensor_copy(MTMP.bitcast(F32R), MT[B:2 * B, :]))
                then(eng.tensor_tensor(MK[1][B:2 * B, :], MT[B:2 * B, :], MTMP, ALU.subtract))

            def start_valid():
                eng.wait_ge(pe_valid, 1)
                eng.tensor_copy(VALID[1][:, :], PS[:, B_Q, B:2 * B])
                eng.tensor_copy(VALID[0][:, :], PS[:, B_Q, 0:B]).then_inc(dve_valid, 1)
                eng.wait_ge(pe_count, 1)
                u = U[:, 0, :]
                then(eng.tensor_scalar(u, PS[:, B_TQ, 0:B], 0.0, HUGE, ALU.is_equal, ALU.mult))
                then(eng.tensor_scalar(u, u, HUGE, 0.0, ALU.mult, ALU.mult))
                eng.wait_ge(dve_valid, 1)
                eng.tensor_tensor(VALID[0][:, :], VALID[0][:, :], u, ALU.add).then_inc(dve_mask, 1)

            def start_cond():
                eng.wait_ge(act_cond, 2)
                for n in range(2):
                    half_c = COND[:, n * D:n * D + D]
                    ins = eng.scalar_tensor_tensor(out=half_c, in0=CTH[n], scalar=1.0, in1=half_c,
                                                   op0=ALU.add, op1=ALU.mult)
                ins.then_inc(dve_cond, 1)
                eng.wait_ge(pe_cond, 1)
                eng.tensor_scalar(CT[:, :, :], PS[:, B_TY, 0:EC * B].rearrange("p (k b) -> p k b", k=EC), 0.5, None,
                                  ALU.mult).then_inc(dve_cond, 1)

            for s in SLOTS:
                i, j, o, m = s, s - 2, s - 3, s + 2
                if s == 0:
                    start_valid()
                    start_cond()
                for w in SPLIT_AT["start"].get(s, []):
                    split_low(w)
                if 0 <= i < NT:
                    keys(i)
                for n in stats_at(s):
                    stat_x(n)
                if m < NSTEP:
                    norm_x(m)
                if s == -2:
                    eng.wait_ge(pe_vec, 1)
                    eng.tensor_copy(VC[:, :], PS[:, B_TY, 0:2 * VROWS]).then_inc(dve_vec, 1)
                    start()
                if 0 <= o < NT:
                    h_mul(o)
                for w in SPLIT_AT["mid"].get(s, []):
                    split_low(w)
                if 0 <= j < NT:
                    attention(j)
                if 0 <= o < NT:
                    h_low(o)
                if 0 <= i < NT:
                    queries(i)
                if 0 <= j < NT:
                    mix(j)
                    norm_y(j)
                if 0 <= o < NT:
                    add_x(o)
                if m < NSTEP:
                    x_low(m)
                if s == -1:
                    start_mask1()
                    for w in range(3):
                        split_low(w)
                if s == 0:
                    split_low(3)
                if film_at(s) is not None:
                    conditioning(film_at(s))
                for w in SPLIT_AT["end"].get(s, []):
                    split_low(w)


def kernel(**inputs):
    import numpy as np
    import concourse.bacc as bacc
    from concourse.bass_utils import run_bass_kernel_spmd

    a = {k: np.asarray(v) for k, v in inputs.items()}
    n0, n1 = "L0_cond_", "L1_cond_"
    names = [
        dict(norm_scale="norm_scale", norm_bias="norm_bias", bk="bk", film_scale="film_norm_scale",
             film_bias="film_norm_bias", film_b="film_emb_b", bv="bv", bq="bq", bo="film_out_b",
             k="Wk", v="Wv", q="Wq", o="film_out_W", film="film_emb_W"),
        dict(norm_scale="ln_w", norm_bias="ln_b", bk="bk", film_scale="ln2_w", film_bias="ln2_b",
             film_b="b_emb", bv="bv", bq="bq", bo="b_out", k="Wk", v="Wv", q="Wq", o="W_out", film="W_emb"),
    ]
    got = [{k: a[p + v] for k, v in n.items()} for p, n in zip((n0, n1), names)]
    arrays = {
        "x": a["x"], "cond": a["cond_2048"],
        "mask0": a["mask_BxS_ik0"], "mask1": a["mask_BxSx1_fk1"].reshape(a["mask_BxS_ik0"].shape),
        "vec_rows": np.concatenate([g[v] for g in got for v in VECTORS]).reshape(-1, P),
        "bias_rows": np.stack([g[v] for g in got for v in ("bv", "bq", "bo")]),
    }
    for l, g in enumerate(got):
        for m in MATS:
            arrays[f"w{m}{l}"] = g[m]
        arrays[f"film{l}"] = g["film"]
    nc = bacc.Bacc("TRN2", target_bir_lowering=False, num_devices=1)
    arrays = {f"in_{k}": np.ascontiguousarray(v) for k, v in arrays.items()}
    ap = {k[3:]: nc.dram_tensor(k, v.shape, mybir.dt.from_np(v.dtype), kind="ExternalInput").ap()
          for k, v in arrays.items()}
    out = nc.dram_tensor("out_x", a["x"].shape, F32, kind="ExternalOutput").ap()
    build_blocks(nc, ap["x"], ap["cond"], ap["mask0"], ap["mask1"],
                 [[ap[f"w{m}{l}"] for m in MATS] for l in range(2)], [ap["film0"], ap["film1"]],
                 ap["vec_rows"], ap["bias_rows"], out)
    r = run_bass_kernel_spmd(nc, [arrays], core_ids=[0])
    return r.results[0]["out_x"]
```

```python
from contextlib import ExitStack

import concourse.bass as bass
from concourse import mybir

F32 = mybir.dt.float32
F32R = mybir.dt.float32r
I32 = mybir.dt.int32
ALU = mybir.AluOpType
ACT = mybir.ActivationFunctionType
AX = mybir.AxisListType

P = 128
VECTORS = ["norm_scale", "norm_bias", "bk", "film_scale", "film_bias", "film_b"]
MATS = ["k", "v", "q", "o"]
EPS = 1e-5
BIG = 2.0 ** 127
HUGE = 3.0e38


def build_blocks(nc, x, cond, mask0, mask1, weights, film_w, vec_rows, bias_rows, out):
    B, T, D = x.shape
    E = cond.shape[1]
    C = D // P
    EC = E // P
    NT = 2 * B
    PAIR = 2 * T
    Q = P // 32
    HEAD = [D // 16, D // 8]
    NSTEP = NT
    VROWS = vec_rows.shape[0] // 2
    assert T == P and C == 4 and E == 2 * D

    row_of, at = {}, 0
    for name in VECTORS:
        row_of[name] = at
        at += (2 * D if name == "film_b" else D) // P
    assert at == VROWS

    ctx = ExitStack()
    with ctx:
        def sb(name, shape, dt=F32):
            return ctx.enter_context(nc.sbuf_tensor(name, shape, dt))

        def sem(name):
            return ctx.enter_context(nc.semaphore(name))

        X = sb("X", [P, B, D])
        WH = [sb(f"WH_{m}", [P, C, D], F32R) for m in MATS]
        WL = [sb(f"WL_{m}", [P, C, D], F32R) for m in MATS]
        STAGE = sb("STAGE", [P, C, D])
        XN = sb("XN", [P, 2, 2 * P])
        XF = sb("XF", [P, 2, PAIR])
        XH = [sb(f"XH{n}", [P, C, PAIR], F32R) for n in range(2)]
        XL = [sb(f"XL{n}", [P, C, PAIR], F32R) for n in range(2)]
        SK = [sb(f"SK{n}", [P, C, PAIR]) for n in range(2)]
        SQ = [sb(f"SQ{n}", [P, D]) for n in range(2)]
        VV = sb("VV", [P, 3, C, P + 1])
        EK = sb("EK", [P, D])
        EQ = sb("EQ", [P, D])
        ATT = sb("ATT", [P, 2, 2 * (P + Q)])
        YN = sb("YN", [P, D])
        Z = sb("Z", [P, D])
        H = sb("H", [P, D])
        HH = sb("HH", [P, D], F32R)
        HL = sb("HL", [P, D], F32R)
        BB = sb("BB", [P, 3, D])
        MK = [sb(f"MK{l}", [P, PAIR], F32R) for l in range(2)]
        SEL = sb("SEL", [P, B // 2], F32R)
        ident = sb("ident", [P, P])
        VALID = [sb(f"VALID{l}", [P, B]) for l in range(2)]
        CT = sb("CT", [P, EC, B])
        G = sb("G", [P, C, B])
        U = sb("U", [P, C, B])
        FA = [sb(f"FA{l}", [P, C, B]) for l in range(2)]
        FC = [sb(f"FC{l}", [P, C, B]) for l in range(2)]
        VC = sb("VC", [P, 2 * VROWS])
        half = sb("half", [P, 1])
        RING = 8
        BNX, BNY = sb("BNX", [P, 6]), sb("BNY", [P, 6])
        MVX = sb("MVX", [P, RING, 2])
        RSX = sb("RSX", [P, RING])
        VEX = sb("VEX", [P, 1])
        MVY = sb("MVY", [P, 2])
        RSY = sb("RSY", [P, 1])
        VEY = sb("VEY", [P, 1])
        KM = sb("KM", [P, 2, 2])
        KB = sb("KB", [P, 2, 2])
        QM = sb("QM", [P, D // min(HEAD)])
        AB = sb("AB", [P, 2, 2, 32])
        RK = sb("RK", [P, 2, 2, 1])
        RQ = sb("RQ", [P, 16])

        ones = EK[:, 0:P]
        VR = H[0:2 * VROWS, 0:P]
        COND = SK[1][0:B, :, :].rearrange("b c n -> b (c n)")
        CTH = [Z[0:B, :], EQ[0:B, :]]
        MI = SQ[1][0:B, 0:T].bitcast(I32)
        MF = SQ[1][0:B, T:2 * T]
        MT = SQ[1][0:B, 2 * T:3 * T]
        MI2 = YN[0:B // 2, 0:PAIR].bitcast(I32)
        MF2 = [YN[32 * n:32 * n + B // 2, PAIR:2 * PAIR] for n in range(2)]
        MT2 = SQ[0][32:32 + B // 2, 0:PAIR]
        MTMP = SQ[0][32:32 + B // 2, PAIR:2 * PAIR]
        STAGES = [STAGE, X[:, 8:12, :], X[:, 12:16, :]] + [STAGE] * 5
        FQ = 2 * D // 4
        FILM0 = X[:, 16:32, :].rearrange("p (k h) n -> p k (h n)", h=2)
        FILM1 = STAGE[:, :, :].rearrange("p c (h n) -> p (c h) n", h=2)

        PS = ctx.enter_context(nc.psum_tensor("PS", [P, 8, 512], F32))
        B_K, B_VO, B_Q, B_XK, B_TQ, B_TY, B_ATT = 0, 1, 2, 3, 4, 5, 6

        XLOADS = [(0, 1), (1, 1), (2, 2), (4, 4), (8, 4), (12, 4), (16, 8), (24, 8)]
        ld_x = [sem(f"ld_x{n}") for n in range(len(XLOADS))]
        ld_w = [sem(f"ld_w{n}") for n in range(8)]
        ld_film = [sem(f"ld_film{n}") for n in range(5)]
        ld_vec, ld_mask, ld_cond = sem("ld_vec"), sem("ld_mask"), sem("ld_cond")
        ld_bias = [sem(f"ld_bias{n}") for n in range(6)]
        st_out = sem("st_out")
        pool_const, pool_x, pool_y = sem("pool_const"), sem("pool_x"), sem("pool_y")
        pool_own, pool_bo = sem("pool_own"), sem("pool_bo")
        pe_vec, pe_cond, pe_valid, pe_count = sem("pe_vec"), sem("pe_cond"), sem("pe_valid"), sem("pe_count")
        pe_k, pe_v, pe_q, pe_o = sem("pe_k"), sem("pe_v"), sem("pe_q"), sem("pe_o")
        pe_tk, pe_tq, pe_ty, pe_a = sem("pe_tk"), sem("pe_tq"), sem("pe_ty"), sem("pe_a")
        pe_att, pe_y, pe_film = sem("pe_att"), sem("pe_y"), sem("pe_film")
        act_cond, act_w = sem("act_cond"), sem("act_w")
        act_ek, act_eq, act_z, act_t = sem("act_ek"), sem("act_eq"), sem("act_z"), sem("act_t")
        act_v, act_hh, act_xf, act_xh = sem("act_v"), sem("act_hh"), sem("act_xf"), sem("act_xh")
        dve_v, dve_q = sem("dve_v"), sem("dve_q")
        dve_vec, dve_const, dve_cond, dve_mask = sem("dve_vec"), sem("dve_const"), sem("dve_cond"), sem("dve_mask")
        dve_w, dve_ks, dve_qs, dve_stat = sem("dve_w"), sem("dve_ks"), sem("dve_qs"), sem("dve_stat")
        dve_xn, dve_xl, dve_x = sem("dve_xn"), sem("dve_xl"), sem("dve_x")
        dve_att, dve_yr, dve_ystat, dve_yn = sem("dve_att"), sem("dve_yr"), sem("dve_ystat"), sem("dve_yn")
        dve_mask_rows, dve_valid = sem("dve_mask_rows"), sem("dve_valid")
        dve_h, dve_hl, dve_film, dve_own = sem("dve_h"), sem("dve_hl"), sem("dve_film"), sem("dve_own")

        def vec(l, name, c0=0, n=C):
            r = l * VROWS + row_of[name] + c0
            return VC[:, r:r + n]

        def x_load_of(tile):
            return next(n for n, (a, k) in enumerate(XLOADS) if a <= tile < a + k)

        def film_at(s):
            return {0: [0], 1: [1], 2: [2, 3], 6: [4], 9: [5], 12: [6], 15: [7]}.get(s, [])

        def stats_at(s):
            return {-2: [0, 1], -1: [2, 3]}.get(s, [s + 4] if s + 4 < NT else [])

        SPLIT_AT = {"mid": {31: [4]}, "end": {31: [5], 34: [7]}, "start": {32: [6]}}
        LAST_USE = {4: pe_k, 5: pe_v, 6: pe_q, 7: pe_o}
        SLOTS = range(-2, NT + 3)

        block = ctx.enter_context(nc.Block())

        @block.sync
        def _(eng):
            def load_x(n):
                a, k = XLOADS[n]
                eng.dma_start(X[:, a:a + k, :], x[a:a + k].rearrange("b t d -> t b d")).then_inc(ld_x[n], 16)

            def load_w(w):
                src = weights[w // 4][w % 4].rearrange("(c p) n -> p c n", p=P)
                eng.dma_start(STAGES[w][:, :, :], src).then_inc(ld_w[w], 16)

            load_x(0)
            load_x(1)
            load_w(0)
            load_w(1)
            load_w(2)
            load_x(2)
            eng.dma_start(FILM0, film_w[0].rearrange("(k p) n -> p k n", p=P)).then_inc(ld_film[0], 16)
            load_x(3)
            eng.wait_ge(dve_w, C)
            load_w(3)
            eng.wait_ge(dve_w, 2 * C)
            load_x(4)
            eng.wait_ge(dve_w, 3 * C)
            load_x(5)
            eng.wait_ge(pe_film, 4)
            load_x(6)
            load_x(7)
            eng.wait_ge(dve_w, 4 * C)
            for n in range(4):
                if n:
                    eng.wait_ge(pe_film, 4 + n)
                eng.dma_start(FILM1, film_w[1].rearrange("(k p) n -> p k n", p=P)[:, :, n * FQ:(n + 1) * FQ])\
                   .then_inc(ld_film[1 + n], 16)
            eng.wait_ge(pe_film, 8)
            load_w(4)
            for r, used in ((0, dve_v), (1, dve_q), (2, pool_bo)):
                if r < 2:
                    eng.wait_ge(dve_w, (5 + r) * C)
                    load_w(5 + r)
                eng.wait_ge(used, B)
                eng.dma_start(BB[:, r, :], bias_rows[3 + r:4 + r].partition_broadcast(P)).then_inc(ld_bias[3 + r], 16)
            eng.wait_ge(dve_w, 7 * C)
            load_w(7)
            for b in range(B):
                eng.wait_ge(dve_x, B + b + 1)
                eng.dma_start(out[b], X[:, b, :]).then_inc(st_out, 16)
            eng.wait_ge(st_out, 16 * B)

        @block.gpsimd
        def _(eng):
            eng.memset(ident[:, :], 0.0).then_inc(pool_own, 1)
            eng.wait_ge(pool_own, 1)
            eng.affine_select(out=ident[:, :], in_=ident[:, :], compare_op=ALU.not_equal, fill=1.0,
                              base=0, pattern=[[-1, P]], channel_multiplier=1).then_inc(pool_const, 1)
            eng.memset(half[:, :], -0.5).then_inc(pool_const, 1)
            eng.memset(ones, 1.0).then_inc(pool_const, 1)
            eng.memset(ATT[:, :, :], 0.0).then_inc(pool_const, 1)
            eng.memset(VV[:, :, :, P:P + 1], 1.0).then_inc(pool_const, 1)
            eng.wait_ge(pool_const, 2)
            own = [1]

            def root(var, plus, out_):
                eng.tensor_scalar(plus, var, EPS, None, ALU.add).then_inc(pool_own, 1)
                own[0] += 1
                eng.wait_ge(pool_own, own[0])
                return eng.tensor_tensor(out_, plus, half[:, :], ALU.pow)

            def root_x(n):
                eng.wait_ge(dve_stat, n + 1)
                root(MVX[:, n % RING, 1:2], VEX[:, :], RSX[:, n % RING:n % RING + 1]).then_inc(pool_x, 1)
                eng.wait_ge(pool_x, n + 1)

            def root_y(j):
                eng.wait_ge(dve_ystat, j + 1)
                root(MVY[:, 1:2], VEY[:, :], RSY[:, :]).then_inc(pool_y, 1)
                eng.wait_ge(pool_y, j + 1)

            def add_bo(i):
                l, b = divmod(i, B)
                eng.wait_ge(dve_xn, 2 * (i // 2) + 2)
                if b == 0:
                    eng.wait_ge(ld_bias[3 * l + 2], 16)
                eng.tensor_tensor(X[:, b, :], X[:, b, :], BB[:, 2, :], ALU.add).then_inc(pool_bo, 1)

            for s in SLOTS:
                for n in stats_at(s):
                    root_x(n)
                if 0 <= s < NT:
                    add_bo(s)
                if 0 <= s - 2 < NT:
                    root_y(s - 2)

        @block.scalar
        def _(eng):
            eng.dma_start(VR, vec_rows).then_inc(ld_vec, 16)
            eng.dma_start(COND, cond).then_inc(ld_cond, 16)
            eng.dma_start(MI, mask0).then_inc(ld_mask, 16)
            eng.dma_start(MF, mask1).then_inc(ld_mask, 16)
            eng.dma_start(MI2, mask0.rearrange("(g t) n -> g (t n)", t=2)).then_inc(ld_mask, 16)
            for n in range(2):
                eng.dma_start(MF2[n], mask1.rearrange("(g t) n -> g (t n)", t=2)).then_inc(ld_mask, 16)
            for r in range(3):
                eng.dma_start(BB[:, r, :], bias_rows[r:r + 1].partition_broadcast(P)).then_inc(ld_bias[r], 16)
            eng.wait_ge(ld_cond, 16)
            for n in range(2):
                eng.activation(CTH[n], COND[:, n * D:n * D + D], ACT.Tanh, scale=0.5).then_inc(act_cond, 1)

            def split_high(w):
                eng.wait_ge(ld_w[w], 16)
                if w in LAST_USE:
                    eng.wait_ge(LAST_USE[w], B)
                for c in range(C):
                    eng.activation(WH[w % 4][:, c, :], STAGES[w][:, c, :], ACT.Copy).then_inc(act_w, 1)

            def exp_k(j):
                eng.wait_ge(pe_tk, j + 1)
                eng.wait_ge(pe_att, j)
                eng.activation(EK[:, :], PS[:, B_XK, :], ACT.Exp).then_inc(act_ek, 1)

            def exp_q(j):
                eng.wait_ge(pe_tq, j + 1)
                eng.wait_ge(pe_y, j)
                eng.activation(EQ[:, :], PS[:, B_TQ, :], ACT.Exp).then_inc(act_eq, 1)

            def film(o):
                l, b = divmod(o, B)
                eng.wait_ge(pe_ty, o + 1)
                eng.wait_ge(dve_film, 4 * (l + 1))
                eng.wait_ge(dve_h, o)
                for c in range(C):
                    z = eng.activation(Z[:, c * P:c * P + P], PS[:, B_TY, c * P:c * P + P], ACT.Identity,
                                       bias=FC[l][:, c, b:b + 1], scale=FA[l][:, c, b:b + 1])
                z.then_inc(act_z, 1)
                eng.wait_ge(act_z, o + 1)
                eng.wait_ge(dve_hl, o)
                eng.activation(H[:, :], Z[:, :], ACT.Tanh).then_inc(act_t, 1)

            def values(i):
                l, b = divmod(i, B)
                eng.wait_ge(dve_v, i + 1)
                eng.wait_ge(dve_mask, 1)
                v = VV[:, i % 3, :, 0:P]
                eng.activation(v, v, ACT.Copy, scale=VALID[l][:, b:b + 1]).then_inc(act_v, 1)

            def h_high(o):
                eng.wait_ge(dve_h, o + 1)
                eng.wait_ge(pe_o, o)
                eng.activation(HH[:, :], H[:, :], ACT.Copy).then_inc(act_hh, 1)

            def x_turned(m):
                g, p = divmod(m, 2)
                l = g // (B // 2)
                eng.wait_ge(pe_a, m + 1)
                if m == 0:
                    eng.wait_ge(dve_vec, 1)
                eng.wait_ge(dve_xl, m)
                eng.wait_ge(act_xh, m)
                for cc in range(2):
                    f = eng.activation(XF[:, cc, :], PS[:, B_XK, cc * PAIR:(cc + 1) * PAIR], ACT.Identity,
                                       bias=vec(l, "norm_bias", 2 * p + cc, 1),
                                       scale=vec(l, "norm_scale", 2 * p + cc, 1))
                f.then_inc(act_xf, 1)
                eng.wait_ge(act_xf, m + 1)
                if g >= 2:
                    eng.wait_ge(pe_q, 2 * g - 2)
                eng.activation(XH[g % 2][:, 2 * p:2 * p + 2, :], XF[:, :, :], ACT.Copy).then_inc(act_xh, 1)

            for s in SLOTS:
                i, j, o, m = s, s - 2, s - 3, s + 2
                for w in SPLIT_AT["start"].get(s, []):
                    split_high(w)
                if 0 <= j < NT:
                    exp_k(j)
                    exp_q(j)
                if 0 <= o < NT:
                    film(o)
                for w in SPLIT_AT["mid"].get(s, []):
                    split_high(w)
                if 0 <= i < NT:
                    values(i)
                if 0 <= o < NT:
                    h_high(o)
                if m < NSTEP:
                    x_turned(m)
                if s == -1:
                    for w in range(3):
                        split_high(w)
                if s == 0:
                    split_high(3)
                for w in SPLIT_AT["end"].get(s, []):
                    split_high(w)

        @block.tensor
        def _(eng):
            def bank(b, a=0, n=512):
                return PS[:, b, a:a + n]

            def weights_ready(w):
                eng.wait_ge(act_w, C * (w + 1))
                eng.wait_ge(dve_w, C * (w + 1))

            def split_product(dst, left, right, first=True, last=True):
                for c in range(C):
                    for a, b in ((0, 0), (0, 1), (1, 0)):
                        mm = eng.matmul(dst, left[a](c), right[b](c), start=(first and c == 0 and a + b == 0),
                                        stop=(last and c == C - 1 and a == 1))
                return mm

            def picked(r):
                return SEL[:, r:r + 1].to_broadcast([P, P])

            def keys(i):
                g, p = divmod(i, 2)
                l = i // B
                eng.wait_ge(act_xh, 2 * g + 2)
                eng.wait_ge(dve_xl, 2 * g + 2)
                eng.wait_ge(dve_ks, i)
                weights_ready(4 * l)
                if i == 0:
                    eng.wait_ge(dve_const, 1)
                xs = [lambda c: XH[g % 2][:, c, :], lambda c: XL[g % 2][:, c, :]]
                for cc in range(2):
                    f = (2 * p + cc) * P
                    ws = [lambda c: WH[0][:, c, f:f + P], lambda c: WL[0][:, c, f:f + P]]
                    dst = bank(B_K, cc * PAIR, PAIR)
                    split_product(dst, ws, xs, last=False)
                    mm = eng.matmul(dst, picked(g % (B // 2)), MK[l][:, :], start=False, stop=True)
                mm.then_inc(pe_k, 1)

            def project_x(i, mat, dst, done):
                l, g, t = i // B, i // 2, i % 2
                xs = [lambda c: XH[g % 2][:, c, t * T:t * T + T], lambda c: XL[g % 2][:, c, t * T:t * T + T]]
                ws = [lambda c: WH[mat][:, c, :], lambda c: WL[mat][:, c, :]]
                weights_ready(4 * l + mat)
                split_product(dst, xs, ws).then_inc(done, 1)

            def values(i):
                eng.wait_ge(dve_v, i)
                if i >= 4:
                    eng.wait_ge(dve_x, i - 3)
                project_x(i, 1, bank(B_VO), pe_v)

            def queries(i):
                eng.wait_ge(dve_q, i)
                eng.wait_ge(dve_film, sum(len(film_at(s)) for s in range(i)))
                project_x(i, 2, bank(B_Q), pe_q)

            def turn_keys(j):
                g, t = divmod(j, 2)
                eng.wait_ge(dve_ks, 2 * g + 2)
                eng.wait_ge(act_xf, min(j + 4, NSTEP))
                for c in range(C):
                    mm = eng.transpose(bank(B_XK, c * P, P), SK[g % 2][:, c, t * T:t * T + T], ident[:, :])
                mm.then_inc(pe_tk, 1)

            def turn_queries(j):
                eng.wait_ge(dve_qs, j + 1)
                eng.wait_ge(act_eq, j)
                for c in range(C):
                    mm = eng.transpose(bank(B_TQ, c * P, P), SQ[j % 2][:, c * P:c * P + P], ident[:, :])
                mm.then_inc(pe_tq, 1)

            def turn_y(o):
                eng.wait_ge(dve_yn, o + 1)
                eng.wait_ge(act_z, o)
                for c in range(C):
                    mm = eng.transpose(bank(B_TY, c * P, P), YN[:, c * P:c * P + P], ident[:, :])
                mm.then_inc(pe_ty, 1)

            def attention(j):
                eng.wait_ge(act_ek, j + 1)
                eng.wait_ge(act_v, j + 1)
                eng.wait_ge(dve_yr, j)
                for c in range(C):
                    mm = eng.matmul(bank(B_ATT + c // 2, (c % 2) * (P + 1), P + 1), EK[:, c * P:c * P + P],
                                    VV[:, j % 3, c, :], start=True, stop=True)
                mm.then_inc(pe_att, 1)

            def mix(j):
                eng.wait_ge(act_eq, j + 1)
                eng.wait_ge(dve_att, j + 1)
                W = P + Q
                for c in range(C):
                    mm = eng.matmul(bank(B_ATT + c // 2, (c % 2) * W, W), EQ[:, c * P:c * P + P],
                                    ATT[:, c // 2, (c % 2) * W:(c % 2 + 1) * W], start=True, stop=True)
                mm.then_inc(pe_y, 1)

            def output(o):
                l = o // B
                eng.wait_ge(act_hh, o + 1)
                eng.wait_ge(dve_hl, o + 1)
                eng.wait_ge(dve_v, min(o + 4, NT))
                weights_ready(4 * l + 3)
                hs = [lambda c: HH[:, c * P:c * P + P], lambda c: HL[:, c * P:c * P + P]]
                ws = [lambda c: WH[3][:, c, :], lambda c: WL[3][:, c, :]]
                split_product(bank(B_VO), hs, ws).then_inc(pe_o, 1)

            def turn_x(m):
                eng.wait_ge(dve_xn, m + 1)
                eng.wait_ge(act_xf, m)
                if m >= 4:
                    eng.wait_ge(act_ek, m - 3)
                for cc in range(2):
                    for t in range(2):
                        mm = eng.transpose(bank(B_XK, cc * PAIR + t * T, T), XN[:, t, cc * P:cc * P + P], ident[:, :])
                mm.then_inc(pe_a, 1)

            def conditioning(n):
                eng.wait_ge(ld_film[0 if n < 4 else n - 3], 16)
                eng.wait_ge(dve_cond, 2)
                eng.wait_ge(dve_film, n)
                w = FILM0[:, :, n * FQ:(n + 1) * FQ] if n < 4 else FILM1
                for c in range(FQ // P):
                    for k in range(EC):
                        mm = eng.matmul(bank(B_Q, c * B, B), w[:, k, c * P:c * P + P], CT[:, k, :],
                                        start=(k == 0), stop=(k == EC - 1))
                mm.then_inc(pe_film, 1)

            eng.wait_ge(pool_const, 5)
            eng.wait_ge(ld_vec, 16)
            n = 2 * VROWS
            eng.transpose(bank(B_TY, 0, n), VR, ident[0:n, 0:n]).then_inc(pe_vec, 1)
            for s in SLOTS:
                i, j, o, m = s, s - 2, s - 3, s + 2
                if s == 0:
                    eng.wait_ge(dve_mask_rows, 1)
                    for l in range(2):
                        mm = eng.transpose(bank(B_Q, l * B, B), MT if l == 0 else MF, ident[0:B, 0:B])
                    mm.then_inc(pe_valid, 1)
                    eng.wait_ge(dve_valid, 1)
                    eng.matmul(bank(B_TQ, 0, B), ones, VALID[0][:, :], start=True, stop=True).then_inc(pe_count, 1)
                    eng.wait_ge(dve_cond, 1)
                    for k in range(EC):
                        mm = eng.transpose(bank(B_TY, k * B, B), COND[:, k * P:k * P + P], ident[0:B, 0:B])
                    mm.then_inc(pe_cond, 1)
                if 0 <= i < NT:
                    keys(i)
                if 0 <= j < NT:
                    turn_keys(j)
                    turn_queries(j)
                if 0 <= o < NT:
                    turn_y(o)
                if 0 <= i < NT:
                    values(i)
                if 0 <= j < NT:
                    attention(j)
                if m < NSTEP:
                    turn_x(m)
                if 0 <= i < NT:
                    queries(i)
                if 0 <= j < NT:
                    mix(j)
                if 0 <= o < NT:
                    output(o)
                for n in film_at(s):
                    eng.wait_ge(dve_q, s + 1)
                    conditioning(n)

        @block.vector
        def _(eng):
            own = [0]

            def then(ins):
                own[0] += 1
                ins.then_inc(dve_own, 1)
                eng.wait_ge(dve_own, own[0])

            def split_low(w):
                eng.wait_ge(ld_w[w], 16)
                for c in range(C):
                    eng.wait_ge(act_w, C * w + c + 1)
                    eng.tensor_tensor(WL[w % 4][:, c, :], STAGES[w][:, c, :], WH[w % 4][:, c, :].bitcast(F32),
                                      ALU.subtract).then_inc(dve_w, 1)

            def stat_x(n):
                if n < B:
                    if n in [a for a, _ in XLOADS]:
                        eng.wait_ge(ld_x[x_load_of(n)], 16)
                else:
                    eng.wait_ge(dve_x, n - B + 1)
                then(eng.bn_stats(BNX[:, :], X[:, n % B, :]))
                if n >= RING:
                    eng.wait_ge(pool_x, n - RING + 1)
                eng.bn_aggr(MVX[:, n % RING, :], BNX[:, :]).then_inc(dve_stat, 1)
                eng.wait_ge(dve_stat, n + 1)

            def norm_x(m):
                g, p = divmod(m, 2)
                eng.wait_ge(pool_x, 2 * g + 2)
                eng.wait_ge(pe_a, m)
                for t in range(2):
                    n = 2 * g + t
                    r = n % RING
                    ins = eng.tensor_scalar(XN[:, t, :], X[:, n % B, 2 * p * P:2 * (p + 1) * P], MVX[:, r, 0:1],
                                            RSX[:, r:r + 1], ALU.subtract, ALU.mult)
                ins.then_inc(dve_xn, 1)

            def x_low(m):
                g, p = divmod(m, 2)
                eng.wait_ge(act_xh, m + 1)
                if g >= 2:
                    eng.wait_ge(pe_q, 2 * g - 2)
                dst = slice(2 * p, 2 * p + 2)
                eng.tensor_tensor(XL[g % 2][:, dst, :], XF[:, :, :], XH[g % 2][:, dst, :].bitcast(F32),
                                  ALU.subtract).then_inc(dve_xl, 1)

            def keys(i):
                l, g, p = i // B, i // 2, i % 2
                eng.wait_ge(pe_k, i + 1)
                ps = PS[:, B_K, :].rearrange("p (c t n) -> p c t n", c=2, t=2)
                then(eng.tensor_reduce(KM[:, :, :].rearrange("p c t -> p (c t)"),
                                       PS[:, B_K, :].rearrange("p (a n) -> p a n", n=T), AX.X, ALU.max))
                bk = vec(l, "bk", 2 * p, 2)
                then(eng.tensor_tensor(KB[:, :, :], KM[:, :, :], bk.unsqueeze(2).to_broadcast([P, 2, 2]), ALU.add))
                if g >= 2:
                    eng.wait_ge(pe_tk, 2 * g - 2)
                for cc in range(2):
                    c = 2 * p + cc
                    ins = eng.scalar_tensor_tensor(
                        out=SK[g % 2][:, c, :].rearrange("p (t n) -> p t n", t=2), in0=ps[:, cc],
                        scalar=bk[:, cc:cc + 1], in1=KB[:, cc, :].unsqueeze(2).to_broadcast([P, 2, T]),
                        op0=ALU.add, op1=ALU.subtract)
                ins.then_inc(dve_ks, 1)

            def queries(i):
                w = HEAD[i // B]
                eng.wait_ge(pe_q, i + 1)
                if i % B == 0:
                    eng.wait_ge(ld_bias[3 * (i // B) + 1], 16)
                if i >= 2:
                    eng.wait_ge(pe_tq, i - 1)
                eng.tensor_tensor(SQ[i % 2][:, :], PS[:, B_Q, :], BB[:, 1, :], ALU.add).then_inc(dve_q, 1)
                eng.wait_ge(dve_q, i + 1)
                sq = SQ[i % 2][:, :].rearrange("p (h n) -> p h n", n=w)
                qm = QM[:, 0:D // w]
                then(eng.tensor_reduce(qm, sq, AX.X, ALU.max))
                eng.tensor_tensor(sq, sq, qm.unsqueeze(2).to_broadcast([P, D // w, w]), ALU.subtract).then_inc(dve_qs, 1)

            def values(i):
                eng.wait_ge(pe_v, i + 1)
                if i % B == 0:
                    eng.wait_ge(ld_bias[3 * (i // B)], 16)
                if i >= 3:
                    eng.wait_ge(pe_att, i - 2)
                eng.tensor_tensor(VV[:, i % 3, :, 0:P], PS[:, B_VO, :].rearrange("p (c n) -> p c n", c=C),
                                  BB[:, 0, :].rearrange("p (c n) -> p c n", c=C), ALU.add).then_inc(dve_v, 1)

            def attention(j):
                l = j // B
                w = HEAD[l]
                eng.wait_ge(pe_att, j + 1)
                eng.wait_ge(pe_y, j)
                if j == B:
                    for h in range(P // w):
                        ATT_h = ATT[h * w:(h + 1) * w, :, :]
                        eng.memset(ATT_h[:, :, 2 * h:2 * h + 2], 1.0)
                        eng.memset(ATT_h[:, :, 2 * P + Q + 2 * h:2 * P + Q + 2 * h + 2], 1.0)
                ps = PS[:, B_ATT:B_ATT + 2, 0:2 * (P + 1)].rearrange("p b (c n) -> p b c n", c=2)
                then(eng.reciprocal(RK[:, :, :, :], ps[:, :, :, P:P + 1]))
                dst = ATT[:, :, Q:Q + 2 * P].rearrange("p b (c n) -> p b c n", c=2)
                for h in range(P // w):
                    a, z = h * w, (h + 1) * w
                    to = AB[a:z, :, :, :] if l == 0 else dst[a:z, :, :, a:z]
                    ins = eng.tensor_tensor(to, ps[a:z, :, :, a:z], RK[a:z, :, :, :].to_broadcast([w, 2, 2, w]),
                                            ALU.mult)
                if l == 0:
                    then(ins)
                    for h in range(P // w):
                        a, z = h * w, (h + 1) * w
                        ins = eng.transpose(dst[a:z, :, :, a:z], AB[a:z, :, :, :])
                ins.then_inc(dve_att, 1)

            def mix(j):
                eng.wait_ge(pe_y, j + 1)
                ps = PS[:, B_ATT:B_ATT + 2, 0:Q]
                sums = bass.AP(tensor=ps.tensor, offset=ps.offset, ap=[ps.ap[0], ps.ap[1], [Q + 2 * P, 2], [1, Q]])
                then(eng.reciprocal(RQ[:, :].rearrange("p (b s q) -> p b s q", b=2, s=2), sums))
                eng.wait_ge(pe_ty, j)
                eng.tensor_tensor(YN[:, :].rearrange("p (b h n) -> p b h n", b=2, n=32),
                                  PS[:, B_ATT:B_ATT + 2, Q:Q + 2 * P].rearrange("p b (h n) -> p b h n", n=32),
                                  RQ[:, :].rearrange("p (b h) -> p b h", b=2).unsqueeze(3).to_broadcast([P, 2, 8, 32]),
                                  ALU.mult).then_inc(dve_yr, 1)
                eng.wait_ge(dve_yr, j + 1)
                then(eng.bn_stats(BNY[:, :], YN[:, :]))
                eng.wait_ge(pool_y, j)
                eng.bn_aggr(MVY[:, :], BNY[:, :]).then_inc(dve_ystat, 1)

            def norm_y(j):
                eng.wait_ge(dve_ystat, j + 1)
                eng.wait_ge(pool_y, j + 1)
                eng.tensor_scalar(YN[:, :], YN[:, :], MVY[:, 0:1], RSY[:, :], ALU.subtract, ALU.mult)\
                   .then_inc(dve_yn, 1)

            def h_mul(o):
                eng.wait_ge(act_t, o + 1)
                eng.scalar_tensor_tensor(out=H[:, :], in0=H[:, :], scalar=1.0, in1=Z[:, :],
                                         op0=ALU.add, op1=ALU.mult).then_inc(dve_h, 1)

            def h_low(o):
                eng.wait_ge(act_hh, o + 1)
                eng.wait_ge(dve_h, o + 1)
                eng.wait_ge(pe_o, o)
                eng.tensor_tensor(HL[:, :], H[:, :], HH[:, :].bitcast(F32), ALU.subtract).then_inc(dve_hl, 1)

            def add_x(o):
                eng.wait_ge(pe_o, o + 1)
                b = o % B
                eng.wait_ge(pool_bo, o + 1)
                eng.tensor_tensor(X[:, b, :], PS[:, B_VO, :], X[:, b, :], ALU.add).then_inc(dve_x, 1)

            def conditioning(n):
                l, h, c0 = n // 4, n // 2 % 2, n % 2 * 2
                eng.wait_ge(pe_film, n + 1)
                ps = PS[:, B_Q, 0:2 * B].rearrange("p (c b) -> p c b", c=2)
                here = slice(c0, c0 + 2)

                def wide(v):
                    return v.unsqueeze(2).to_broadcast([P, 2, B])

                if h == 0:
                    then(eng.scalar_tensor_tensor(out=G[:, here, :], in0=ps, scalar=1.0,
                                                  in1=wide(vec(l, "film_b", c0, 2)), op0=ALU.add, op1=ALU.add))
                    last = eng.scalar_tensor_tensor(out=FA[l][:, here, :], in0=G[:, here, :], scalar=0.5,
                                                    in1=wide(vec(l, "film_scale", c0, 2)), op0=ALU.mult, op1=ALU.mult)
                else:
                    then(eng.tensor_tensor(U[:, here, :], ps, wide(vec(l, "film_b", C + c0, 2)), ALU.add))
                    then(eng.tensor_tensor(G[:, here, :], G[:, here, :], wide(vec(l, "film_bias", c0, 2)), ALU.mult))
                    then(eng.tensor_tensor(G[:, here, :], G[:, here, :], U[:, here, :], ALU.add))
                    last = eng.tensor_scalar(FC[l][:, here, :], G[:, here, :], 0.5, None, ALU.mult)
                last.then_inc(dve_film, 1)

            def start():
                eng.wait_ge(pool_const, 5)
                for g in range(Q):
                    a, z = 32 * g, 32 * g + 32
                    eng.memset(ATT[a:z, :, g:g + 1], 1.0)
                    eng.memset(ATT[a:z, :, 2 * P + Q + g:2 * P + Q + g + 1], 1.0)
                then(eng.memset(MK[0][:, :].bitcast(F32), 0.0))
                then(eng.memset(MK[1][:, :].bitcast(F32), 0.0))
                eng.tensor_tensor(SEL[:, :], ident[:, 0:B // 2], ident[:, 32:32 + B // 2], ALU.add)
                eng.wait_ge(ld_mask, 80)
                eng.tensor_scalar(MT, MI, 1.0, None, ALU.not_equal).then_inc(dve_mask_rows, 1)
                n = B // 2
                eng.tensor_scalar(MK[0][0:n, :], MI2, 1.0, -BIG, ALU.is_equal, ALU.mult)
                eng.tensor_scalar(MK[1][0:n, :], MF2[0], 1.0, 1.0e6, ALU.subtract, ALU.mult)
                then(eng.tensor_scalar(MT2, MF2[1], 1.0, 1.0e6, ALU.subtract, ALU.mult))
                then(eng.tensor_copy(MTMP.bitcast(F32R), MT2))
                eng.tensor_tensor(MK[1][32:32 + n, :], MT2, MTMP, ALU.subtract).then_inc(dve_const, 1)

            def start_valid():
                eng.wait_ge(pe_valid, 1)
                eng.tensor_copy(VALID[1][:, :], PS[:, B_Q, B:2 * B])
                eng.tensor_copy(VALID[0][:, :], PS[:, B_Q, 0:B]).then_inc(dve_valid, 1)
                eng.wait_ge(pe_count, 1)
                u = U[:, 0, :]
                then(eng.tensor_scalar(u, PS[:, B_TQ, 0:B], 0.0, HUGE, ALU.is_equal, ALU.mult))
                then(eng.tensor_scalar(u, u, HUGE, 0.0, ALU.mult, ALU.mult))
                eng.wait_ge(dve_valid, 1)
                eng.tensor_tensor(VALID[0][:, :], VALID[0][:, :], u, ALU.add).then_inc(dve_mask, 1)

            def start_cond():
                eng.wait_ge(act_cond, 2)
                for n in range(2):
                    half_c = COND[:, n * D:n * D + D]
                    ins = eng.scalar_tensor_tensor(out=half_c, in0=CTH[n], scalar=1.0, in1=half_c,
                                                   op0=ALU.add, op1=ALU.mult)
                ins.then_inc(dve_cond, 1)
                eng.wait_ge(pe_cond, 1)
                eng.tensor_scalar(CT[:, :, :], PS[:, B_TY, 0:EC * B].rearrange("p (k b) -> p k b", k=EC), 0.5, None,
                                  ALU.mult).then_inc(dve_cond, 1)

            for s in SLOTS:
                i, j, o, m = s, s - 2, s - 3, s + 2
                if s == 0:
                    start_valid()
                    start_cond()
                for w in SPLIT_AT["start"].get(s, []):
                    split_low(w)
                if 0 <= i < NT:
                    keys(i)
                for n in stats_at(s):
                    stat_x(n)
                if m < NSTEP:
                    norm_x(m)
                if s == -2:
                    eng.wait_ge(pe_vec, 1)
                    eng.tensor_copy(VC[:, :], PS[:, B_TY, 0:2 * VROWS]).then_inc(dve_vec, 1)
                    start()
                if 0 <= o < NT:
                    h_mul(o)
                for w in SPLIT_AT["mid"].get(s, []):
                    split_low(w)
                if 0 <= i < NT:
                    values(i)
                if 0 <= j < NT:
                    attention(j)
                if 0 <= o < NT:
                    h_low(o)
                if m < NSTEP:
                    x_low(m)
                if 0 <= i < NT:
                    queries(i)
                if 0 <= j < NT:
                    mix(j)
                    norm_y(j)
                if 0 <= o < NT:
                    add_x(o)
                if s == -1:
                    for w in range(3):
                        split_low(w)
                if s == 0:
                    split_low(3)
                for n in film_at(s):
                    conditioning(n)
                for w in SPLIT_AT["end"].get(s, []):
                    split_low(w)


def kernel(**inputs):
    import numpy as np
    import concourse.bacc as bacc
    from concourse.bass_utils import run_bass_kernel_spmd

    a = {k: np.asarray(v) for k, v in inputs.items()}
    n0, n1 = "L0_cond_", "L1_cond_"
    names = [
        dict(norm_scale="norm_scale", norm_bias="norm_bias", bk="bk", film_scale="film_norm_scale",
             film_bias="film_norm_bias", film_b="film_emb_b", bv="bv", bq="bq", bo="film_out_b",
             k="Wk", v="Wv", q="Wq", o="film_out_W", film="film_emb_W"),
        dict(norm_scale="ln_w", norm_bias="ln_b", bk="bk", film_scale="ln2_w", film_bias="ln2_b",
             film_b="b_emb", bv="bv", bq="bq", bo="b_out", k="Wk", v="Wv", q="Wq", o="W_out", film="W_emb"),
    ]
    got = [{k: a[p + v] for k, v in n.items()} for p, n in zip((n0, n1), names)]
    arrays = {
        "x": a["x"], "cond": a["cond_2048"],
        "mask0": a["mask_BxS_ik0"], "mask1": a["mask_BxSx1_fk1"].reshape(a["mask_BxS_ik0"].shape),
        "vec_rows": np.concatenate([g[v] for g in got for v in VECTORS]).reshape(-1, P),
        "bias_rows": np.stack([g[v] for g in got for v in ("bv", "bq", "bo")]),
    }
    for l, g in enumerate(got):
        for m in MATS:
            arrays[f"w{m}{l}"] = g[m]
        arrays[f"film{l}"] = g["film"]
    nc = bacc.Bacc("TRN2", target_bir_lowering=False, num_devices=1)
    arrays = {f"in_{k}": np.ascontiguousarray(v) for k, v in arrays.items()}
    ap = {k[3:]: nc.dram_tensor(k, v.shape, mybir.dt.from_np(v.dtype), kind="ExternalInput").ap()
          for k, v in arrays.items()}
    out = nc.dram_tensor("out_x", a["x"].shape, F32, kind="ExternalOutput").ap()
    build_blocks(nc, ap["x"], ap["cond"], ap["mask0"], ap["mask1"],
                 [[ap[f"w{m}{l}"] for m in MATS] for l in range(2)], [ap["film0"], ap["film1"]],
                 ap["vec_rows"], ap["bias_rows"], out)
    r = run_bass_kernel_spmd(nc, [arrays], core_ids=[0])
    return r.results[0]["out_x"]
```

```python
from contextlib import ExitStack

import concourse.bass as bass
from concourse import mybir

F32 = mybir.dt.float32
F32R = mybir.dt.float32r
I32 = mybir.dt.int32
ALU = mybir.AluOpType
ACT = mybir.ActivationFunctionType
AX = mybir.AxisListType

P = 128
VECTORS = ["norm_scale", "norm_bias", "bk", "film_scale", "film_bias", "film_b"]
MATS = ["k", "v", "q", "o"]
EPS = 1e-5
BIG = 2.0 ** 127
HUGE = 3.0e38


def build_blocks(nc, x, cond, mask0, mask1, weights, film_w, vec_rows, bias_rows, out):
    B, T, D = x.shape
    E = cond.shape[1]
    C = D // P
    EC = E // P
    NT = 2 * B
    PAIR = 2 * T
    Q = P // 32
    HEAD = [D // 16, D // 8]
    NSTEP = NT
    VROWS = vec_rows.shape[0] // 2
    assert T == P and C == 4 and E == 2 * D

    row_of, at = {}, 0
    for name in VECTORS:
        row_of[name] = at
        at += (2 * D if name == "film_b" else D) // P
    assert at == VROWS

    ctx = ExitStack()
    with ctx:
        def sb(name, shape, dt=F32):
            return ctx.enter_context(nc.sbuf_tensor(name, shape, dt))

        def sem(name):
            return ctx.enter_context(nc.semaphore(name))

        X = sb("X", [P, B, D])
        WH = [sb(f"WH_{m}", [P, C, D], F32R) for m in MATS]
        WL = [sb(f"WL_{m}", [P, C, D], F32R) for m in MATS]
        STAGE = sb("STAGE", [P, C, D])
        XN = sb("XN", [P, 2, 2 * P])
        XF = sb("XF", [P, 2, PAIR])
        XH = [sb(f"XH{n}", [P, C, PAIR], F32R) for n in range(2)]
        XL = [sb(f"XL{n}", [P, C, PAIR], F32R) for n in range(2)]
        SK = [sb(f"SK{n}", [P, C, PAIR]) for n in range(2)]
        SQ = [sb(f"SQ{n}", [P, D]) for n in range(2)]
        VV = sb("VV", [P, 3, D + 16])
        EK = sb("EK", [P, D])
        EQ = sb("EQ", [P, D])
        ATT = sb("ATT", [P, 2, 2 * (P + Q)])
        YN = sb("YN", [P, D])
        Z = sb("Z", [P, D])
        H = sb("H", [P, D])
        HH = sb("HH", [P, D], F32R)
        HL = sb("HL", [P, D], F32R)
        BB = sb("BB", [P, 3, D])
        MB = [sb(f"MB{n}", [P, PAIR]) for n in range(2)]
        ident = sb("ident", [P, P])
        VALID = [sb(f"VALID{l}", [P, B]) for l in range(2)]
        CT = sb("CT", [P, EC, B])
        G = sb("G", [P, C, B])
        U = sb("U", [P, C, B])
        FA = [sb(f"FA{l}", [P, C, B]) for l in range(2)]
        FC = [sb(f"FC{l}", [P, C, B]) for l in range(2)]
        VC = sb("VC", [P, 2 * VROWS])
        CP = sb("CP", [P, D])
        FOLD = sb("FOLD", [P, B])
        half = sb("half", [P, 1])
        RING = 8
        BNX, BNY = sb("BNX", [P, 6]), sb("BNY", [P, 6])
        MVX = sb("MVX", [P, RING, 2])
        RSX = sb("RSX", [P, RING])
        VEX = sb("VEX", [P, 1])
        MVY = sb("MVY", [P, 2])
        RSY = sb("RSY", [P, 1])
        VEY = sb("VEY", [P, 1])
        KM = sb("KM", [P, 2, 2])
        KB = sb("KB", [P, 2, 2])
        QM = sb("QM", [P, D // min(HEAD)])
        AB = sb("AB", [P, C, 32])
        RK = sb("RK", [P, C, 1])
        RQ = sb("RQ", [P, 16])

        ones = EK[:, 0:P]
        VR = H[0:2 * VROWS, 0:P]
        COND = SK[1][0:B, :, :].rearrange("b c n -> b (c n)")
        CTH = [Z[0:B, :], EQ[0:B, :]]
        MI = SQ[1][0:B, 0:T].bitcast(I32)
        MF = SQ[1][0:B, T:2 * T]
        MT = SQ[1][0:B, 2 * T:3 * T]
        STAGES = [STAGE, X[:, 8:12, :], X[:, 12:16, :]] + [STAGE] * 5
        FQ = 2 * D // 4
        FILM0 = X[:, 16:32, :].rearrange("p (k h) n -> p k (h n)", h=2)
        FILM1 = STAGE[:, :, :].rearrange("p c (h n) -> p (c h) n", h=2)

        PS = ctx.enter_context(nc.psum_tensor("PS", [P, 8, 512], F32))
        B_K, B_VO, B_Q, B_XK, B_TQ, B_TY, B_ATT = 0, 1, 2, 3, 4, 5, 6

        XLOADS = [(0, 1), (1, 1), (2, 2), (4, 4), (8, 4), (12, 4), (16, 8), (24, 8)]
        ld_x = [sem(f"ld_x{n}") for n in range(len(XLOADS))]
        ld_w = [sem(f"ld_w{n}") for n in range(4)]
        ld_wc = [[sem(f"ld_w{n}_{c}") for c in range(C)] for n in range(4, 8)]
        low_w = [[sem(f"low_w{n}_{c}") for c in range(C)] for n in range(8)]
        ld_film = [sem(f"ld_film{n}") for n in range(6)]
        ld_vec, ld_mask, ld_cond = sem("ld_vec"), sem("ld_mask"), sem("ld_cond")
        ld_bias = [sem(f"ld_bias{n}") for n in range(6)]
        ld_mb = [sem(f"ld_mb{n}") for n in range(2)]
        st_out = sem("st_out")
        pool_const, pool_x, pool_y = sem("pool_const"), sem("pool_x"), sem("pool_y")
        pool_own, pool_bo = sem("pool_own"), sem("pool_bo")
        pool_mb, pool_q = sem("pool_mb"), sem("pool_q")
        pe_vec, pe_cond, pe_valid, pe_count = sem("pe_vec"), sem("pe_cond"), sem("pe_valid"), sem("pe_count")
        pe_k, pe_v, pe_q, pe_o = sem("pe_k"), sem("pe_v"), sem("pe_q"), sem("pe_o")
        pe_tk, pe_tq, pe_ty, pe_a = sem("pe_tk"), sem("pe_tq"), sem("pe_ty"), sem("pe_a")
        pe_att, pe_y, pe_film = sem("pe_att"), sem("pe_y"), sem("pe_film")
        pe_fold, act_cp = sem("pe_fold"), sem("act_cp")
        act_cond, act_w = sem("act_cond"), sem("act_w")
        act_ek, act_eq, act_z, act_t = sem("act_ek"), sem("act_eq"), sem("act_z"), sem("act_t")
        act_v, act_hh, act_xf, act_xh = sem("act_v"), sem("act_hh"), sem("act_xf"), sem("act_xh")
        dve_v, dve_q = sem("dve_v"), sem("dve_q")
        dve_vec, dve_cond, dve_mask = sem("dve_vec"), sem("dve_cond"), sem("dve_mask")
        dve_ks, dve_qm, dve_stat = sem("dve_ks"), sem("dve_qm"), sem("dve_stat")
        dve_xn, dve_xl, dve_x = sem("dve_xn"), sem("dve_xl"), sem("dve_x")
        dve_att, dve_yr, dve_ystat, dve_yn = sem("dve_att"), sem("dve_yr"), sem("dve_ystat"), sem("dve_yn")
        dve_mask_rows, dve_valid = sem("dve_mask_rows"), sem("dve_valid")
        dve_h, dve_hl, dve_film, dve_own = sem("dve_h"), sem("dve_hl"), sem("dve_film"), sem("dve_own")

        def vec(l, name, c0=0, n=C):
            r = l * VROWS + row_of[name] + c0
            return VC[:, r:r + n]

        def x_load_of(tile):
            return next(n for n, (a, k) in enumerate(XLOADS) if a <= tile < a + k)

        FILM_STEPS = [(0, 0, D), (0, D, D)] + [(1, n * FQ, FQ) for n in range(4)]
        FILM_SLOTS = [1, 2, 6, 9, 12, 15]

        def stats_at(s):
            return [s + 4] if s + 4 < NT else []

        LOW_ON_DVE = [range(C), range(C), [3], [], range(2), range(2, C), range(C), []]
        SPLIT_MID, SPLIT_LATE, SPLIT_END = {31: [4], 32: [6]}, {31: [5]}, {1: [3], 34: [7]}
        LAST_USE = {4: pe_k, 5: pe_v, 6: pe_q, 7: pe_o}
        SLOTS = range(NT)

        t0, t1, t2 = NT - 3, NT - 2, NT - 1
        DRAIN = [("turn", t1), ("attention", t1), ("heads", t1), ("turn_y", t0), ("turn", t2), ("film", t0),
                 ("mix", t1), ("y", t1), ("attention", t2), ("heads", t2), ("h", t0), ("norm_y", t1), ("mix", t2),
                 ("turn_y", t1), ("film", t1), ("h_low", t0), ("output", t0), ("y", t2), ("h", t1), ("norm_y", t2),
                 ("turn_y", t2), ("film", t2), ("h_low", t1), ("output", t1), ("add_x", t0), ("h", t2),
                 ("add_x", t1), ("h_low", t2), ("output", t2), ("add_x", t2)]

        def bank_out(o):
            return {t1: B_K, t2: B_Q}.get(o, B_VO)

        def with_ones(l, i):
            n = HEAD[l] * (D + 16) // D
            return VV[:, i % 3, :].rearrange("p (h n) -> p h n", n=n)[:, :, 0:1 + HEAD[l]]

        def wait_weights(eng, w, c):
            if w >= 4:
                eng.wait_ge(ld_wc[w - 4][c], 16)
            elif c == 0:
                eng.wait_ge(ld_w[w], 16)

        def low_on_pool(w):
            return [c for c in range(C) if c not in LOW_ON_DVE[w]]

        def split_low(eng, w, chunks):
            for c in chunks:
                wait_weights(eng, w, c)
                eng.wait_ge(act_w, C * w + c + 1)
                eng.tensor_tensor(WL[w % 4][:, c, :], STAGES[w][:, c, :], WH[w % 4][:, c, :].bitcast(F32),
                                  ALU.subtract).then_inc(low_w[w][c], 1)

        def load_mask(eng, g):
            l, r = divmod(g, B // 2)
            src = (mask0, mask1)[l].rearrange("(g t) n -> g (t n)", t=2)[r:r + 1]
            dst = MB[g % 2][:, :].bitcast(I32) if l == 0 else MB[g % 2][:, :]
            eng.dma_start(dst, src.partition_broadcast(P)).then_inc(ld_mb[g % 2], 16)

        block = ctx.enter_context(nc.Block())

        @block.sync
        def _(eng):
            def load_x(n):
                a, k = XLOADS[n]
                eng.dma_start(X[:, a:a + k, :], x[a:a + k].rearrange("b t d -> t b d")).then_inc(ld_x[n], 16)

            def load_w(w):
                src = weights[w // 4][w % 4].rearrange("(c p) n -> p c n", p=P)
                if w < 4:
                    eng.dma_start(STAGES[w][:, :, :], src).then_inc(ld_w[w], 16)
                else:
                    for c in range(C):
                        if w > 4:
                            eng.wait_ge(low_w[w - 1][c], 1)
                        eng.dma_start(STAGE[:, c, :], src[:, c, :]).then_inc(ld_wc[w - 4][c], 16)

            def load_film(n):
                l, a, k = FILM_STEPS[n]
                dst = FILM0[:, :, a:a + k] if l == 0 else FILM1
                eng.dma_start(dst, film_w[l].rearrange("(k p) n -> p k n", p=P)[:, :, a:a + k]).then_inc(ld_film[n], 16)

            def wait_split(w):
                for c in range(C):
                    eng.wait_ge(low_w[w][c], 1)

            def load_second_bias(r, used):
                eng.wait_ge(used, B)
                eng.dma_start(BB[:, r, :], bias_rows[3 + r:4 + r].partition_broadcast(P)).then_inc(ld_bias[3 + r], 16)

            def store(b):
                eng.wait_ge(dve_x, B + b + 1)
                eng.dma_start(out[b], X[:, b, :]).then_inc(st_out, 16)

            load_x(0)
            load_x(1)
            load_w(0)
            load_w(1)
            load_w(2)
            load_x(2)
            for r in range(3):
                eng.dma_start(BB[:, r, :], bias_rows[r:r + 1].partition_broadcast(P)).then_inc(ld_bias[r], 16)
            load_film(0)
            load_x(3)
            load_film(1)
            wait_split(0)
            load_w(3)
            wait_split(1)
            load_x(4)
            wait_split(2)
            load_x(5)
            for s in range(1, NT):
                if s % 2 == 0 and s + 2 < NT:
                    eng.wait_ge(dve_ks, s)
                    load_mask(eng, s // 2 + 1)
                if s == 3:
                    eng.wait_ge(pe_film, 2)
                    load_x(6)
                    load_x(7)
                    wait_split(3)
                for n in range(2, 6):
                    if s == FILM_SLOTS[n - 1] + 1:
                        eng.wait_ge(pe_film, n)
                        load_film(n)
                if s == FILM_SLOTS[-1] + 1:
                    eng.wait_ge(pe_film, 6)
                    load_w(4)
                if s == B - 1:
                    load_w(5)
                    load_second_bias(0, dve_v)
                    load_second_bias(2, pool_bo)
                    load_w(6)
                    load_second_bias(1, dve_q)
                    load_w(7)
                if s >= B + 4:
                    store(s - B - 4)
            for b in range(B - 4, B):
                store(b)
            eng.wait_ge(st_out, 16 * B)

        @block.gpsimd
        def _(eng):
            eng.memset(ident[:, :], 0.0).then_inc(pool_own, 1)
            eng.wait_ge(pool_own, 1)
            eng.affine_select(out=ident[:, :], in_=ident[:, :], compare_op=ALU.not_equal, fill=1.0,
                              base=0, pattern=[[-1, P]], channel_multiplier=1).then_inc(pool_const, 1)
            eng.memset(half[:, :], -0.5).then_inc(pool_const, 1)
            eng.memset(ones, 1.0).then_inc(pool_const, 1)
            eng.memset(ATT[:, :, :], 0.0).then_inc(pool_const, 1)
            eng.memset(VV[:, :, :].rearrange("p a (h n) -> p (a h) n", n=HEAD[0] + 1)[:, :, 0:1], 1.0)\
               .then_inc(pool_const, 1)
            eng.wait_ge(pool_const, 2)
            own = [1]

            def root(var, plus, out_):
                eng.tensor_scalar(plus, var, EPS, None, ALU.add).then_inc(pool_own, 1)
                own[0] += 1
                eng.wait_ge(pool_own, own[0])
                return eng.tensor_tensor(out_, plus, half[:, :], ALU.pow)

            def root_x(n):
                eng.wait_ge(dve_stat, n + 1)
                root(MVX[:, n % RING, 1:2], VEX[:, :], RSX[:, n % RING:n % RING + 1]).then_inc(pool_x, 1)
                eng.wait_ge(pool_x, n + 1)

            def root_y(j):
                eng.wait_ge(dve_ystat, j + 1)
                root(MVY[:, 1:2], VEY[:, :], RSY[:, :]).then_inc(pool_y, 1)
                eng.wait_ge(pool_y, j + 1)

            def add_bo(i):
                l, b = divmod(i, B)
                eng.wait_ge(dve_xn, 2 * (i // 2) + 2)
                if b == 0:
                    eng.wait_ge(ld_bias[3 * l + 2], 16)
                eng.tensor_tensor(X[:, b, :], X[:, b, :], BB[:, 2, :], ALU.add).then_inc(pool_bo, 1)

            def queries(i):
                w = HEAD[i // B]
                eng.wait_ge(dve_qm, i + 1)
                sq = SQ[i % 2][:, :].rearrange("p (h n) -> p h n", n=w)
                eng.tensor_tensor(sq, sq, QM[:, 0:D // w].unsqueeze(2).to_broadcast([P, D // w, w]), ALU.subtract)\
                   .then_inc(pool_q, 1)

            def mask_of_keys(g):
                eng.wait_ge(ld_mb[g % 2], 16 * (g // 2 + 1))
                mb = MB[g % 2][:, :]
                if g < B // 2:
                    ins = eng.tensor_scalar(mb, mb.bitcast(I32), 1.0, -BIG, ALU.is_equal, ALU.mult)
                else:
                    ins = eng.tensor_scalar(mb, mb, 1.0, 1.0e6, ALU.subtract, ALU.mult)
                ins.then_inc(pool_mb, 1)

            root_x(0)
            root_x(1)
            mask_of_keys(0)
            split_low(eng, 2, low_on_pool(2))
            root_x(2)
            root_x(3)
            for s in SLOTS:
                for n in stats_at(s):
                    root_x(n)
                if 0 <= s < NT:
                    add_bo(s)
                if s % 2 == 1 and s + 1 < NT:
                    mask_of_keys((s + 1) // 2)
                for w in SPLIT_MID.get(s, []) + SPLIT_LATE.get(s, []):
                    split_low(eng, w, low_on_pool(w))
                if s - 2 >= 0:
                    root_y(s - 2)
                queries(s)
                for w in SPLIT_END.get(s, []):
                    split_low(eng, w, low_on_pool(w))
            root_y(NT - 2)
            root_y(NT - 1)

        @block.scalar
        def _(eng):
            eng.dma_start(VR, vec_rows).then_inc(ld_vec, 16)
            load_mask(eng, 0)
            eng.dma_start(COND, cond).then_inc(ld_cond, 16)
            eng.dma_start(MI, mask0).then_inc(ld_mask, 16)
            eng.dma_start(MF, mask1).then_inc(ld_mask, 16)
            load_mask(eng, 1)

            def split_high(w, chunks=range(C)):
                if w in LAST_USE:
                    eng.wait_ge(LAST_USE[w], B)
                for c in chunks:
                    wait_weights(eng, w, c)
                    eng.activation(WH[w % 4][:, c, :], STAGES[w][:, c, :], ACT.Copy).then_inc(act_w, 1)

            def exp_k(j):
                eng.wait_ge(pe_tk, j + 1)
                eng.wait_ge(pe_att, j)
                eng.activation(EK[:, :], PS[:, B_XK, :], ACT.Exp).then_inc(act_ek, 1)

            def exp_q(j):
                eng.wait_ge(pe_tq, j + 1)
                eng.wait_ge(pe_y, j)
                eng.activation(EQ[:, :], PS[:, B_TQ, :], ACT.Exp).then_inc(act_eq, 1)

            def film(o):
                l, b = divmod(o, B)
                eng.wait_ge(pe_ty, o + 1)
                eng.wait_ge(dve_film, 2 if l == 0 else 6)
                eng.wait_ge(dve_h, o)
                for c in range(C):
                    z = eng.activation(Z[:, c * P:c * P + P], PS[:, B_TY, c * P:c * P + P], ACT.Identity,
                                       bias=FC[l][:, c, b:b + 1], scale=FA[l][:, c, b:b + 1])
                z.then_inc(act_z, 1)
                eng.wait_ge(act_z, o + 1)
                eng.wait_ge(dve_hl, o)
                eng.activation(H[:, :], Z[:, :], ACT.Tanh).then_inc(act_t, 1)

            def values(i):
                l, b = divmod(i, B)
                eng.wait_ge(dve_v, i + 1)
                eng.wait_ge(dve_mask, 1)
                v = with_ones(l, i)[:, :, 1:]
                eng.activation(v, v, ACT.Copy, scale=VALID[l][:, b:b + 1]).then_inc(act_v, 1)

            def conditioning_sums(n):
                k = FILM_STEPS[n][2]
                eng.wait_ge(pe_film, n + 1)
                eng.wait_ge(pe_fold, n)
                eng.activation(CP[:, 0:k], PS[:, B_Q, 0:k], ACT.Copy).then_inc(act_cp, 1)

            def h_high(o):
                eng.wait_ge(dve_h, o + 1)
                eng.wait_ge(pe_o, o)
                eng.activation(HH[:, :], H[:, :], ACT.Copy).then_inc(act_hh, 1)

            def x_turned(m):
                g, p = divmod(m, 2)
                l = g // (B // 2)
                eng.wait_ge(pe_a, m + 1)
                if m == 0:
                    eng.wait_ge(dve_vec, 1)
                eng.wait_ge(dve_xl, m)
                eng.wait_ge(act_xh, m)
                for cc in range(2):
                    f = eng.activation(XF[:, cc, :], PS[:, B_XK, cc * PAIR:(cc + 1) * PAIR], ACT.Identity,
                                       bias=vec(l, "norm_bias", 2 * p + cc, 1),
                                       scale=vec(l, "norm_scale", 2 * p + cc, 1))
                f.then_inc(act_xf, 1)
                eng.wait_ge(act_xf, m + 1)
                if g >= 2:
                    eng.wait_ge(pe_q, 2 * g - 2)
                eng.activation(XH[g % 2][:, 2 * p:2 * p + 2, :], XF[:, :, :], ACT.Copy).then_inc(act_xh, 1)

            x_turned(0)
            split_high(0, range(2))
            x_turned(1)
            split_high(0, range(2, C))
            split_high(1)
            eng.wait_ge(ld_cond, 16)
            for n in range(2):
                eng.activation(CTH[n], COND[:, n * D:n * D + D], ACT.Tanh, scale=0.5).then_inc(act_cond, 1)
            split_high(2)
            for s in SLOTS:
                i, j, o, m = s, s - 2, s - 3, s + 2
                if s in FILM_SLOTS:
                    conditioning_sums(FILM_SLOTS.index(s))
                if 0 <= j < NT:
                    exp_k(j)
                    exp_q(j)
                if 0 <= o < NT:
                    film(o)
                for w in SPLIT_MID.get(s, []):
                    split_high(w)
                if 0 < i < NT:
                    values(i)
                if 0 <= o < NT:
                    h_high(o)
                if m < NSTEP:
                    x_turned(m)
                if s == 0:
                    values(0)
                for w in SPLIT_LATE.get(s, []) + SPLIT_END.get(s, []):
                    split_high(w)

            for stage, n in DRAIN:
                if stage == "turn":
                    exp_k(n)
                    exp_q(n)
                elif stage == "film":
                    film(n)
                elif stage == "h":
                    h_high(n)

        @block.tensor
        def _(eng):
            def bank(b, a=0, n=512):
                return PS[:, b, a:a + n]

            def split_product(dst, left, right, fresh=None):
                for c in range(C):
                    if fresh is not None:
                        eng.wait_ge(low_w[fresh][c], 1)
                    for a, b in ((0, 0), (0, 1), (1, 0)):
                        mm = eng.matmul(dst, left[a](c), right[b](c), start=(c == 0 and a + b == 0),
                                        stop=(c == C - 1 and a == 1))
                return mm

            def keys(i):
                g, p = divmod(i, 2)
                l = i // B
                eng.wait_ge(act_xh, 2 * g + 2)
                eng.wait_ge(dve_xl, 2 * g + 2)
                eng.wait_ge(dve_ks, i)
                xs = [lambda c: XH[g % 2][:, c, :], lambda c: XL[g % 2][:, c, :]]
                for cc in range(2):
                    f = (2 * p + cc) * P
                    ws = [lambda c: WH[0][:, c, f:f + P], lambda c: WL[0][:, c, f:f + P]]
                    dst = bank(B_K, cc * PAIR, PAIR)
                    mm = split_product(dst, ws, xs, fresh=(4 * l if i % B == 0 and cc == 0 else None))
                mm.then_inc(pe_k, 1)

            def project_x(i, mat, dst, done):
                l, g, t = i // B, i // 2, i % 2
                xs = [lambda c: XH[g % 2][:, c, t * T:t * T + T], lambda c: XL[g % 2][:, c, t * T:t * T + T]]
                ws = [lambda c: WH[mat][:, c, :], lambda c: WL[mat][:, c, :]]
                split_product(dst, xs, ws, fresh=(4 * l + mat if i % B == 0 else None)).then_inc(done, 1)

            def values(i):
                eng.wait_ge(dve_v, i)
                if i >= 4:
                    eng.wait_ge(dve_x, i - 3)
                project_x(i, 1, bank(B_VO), pe_v)

            def queries(i):
                eng.wait_ge(dve_q, i)
                eng.wait_ge(act_cp, sum(s <= i for s in FILM_SLOTS))
                project_x(i, 2, bank(B_Q), pe_q)

            def turn_keys(j):
                g, t = divmod(j, 2)
                eng.wait_ge(dve_ks, 2 * g + 2)
                eng.wait_ge(act_xf, min(j + 4, NSTEP))
                for c in range(C):
                    mm = eng.transpose(bank(B_XK, c * P, P), SK[g % 2][:, c, t * T:t * T + T], ident[:, :])
                mm.then_inc(pe_tk, 1)

            def turn_queries(j):
                eng.wait_ge(pool_q, j + 1)
                eng.wait_ge(act_eq, j)
                for c in range(C):
                    mm = eng.transpose(bank(B_TQ, c * P, P), SQ[j % 2][:, c * P:c * P + P], ident[:, :])
                mm.then_inc(pe_tq, 1)

            def turn_y(o):
                eng.wait_ge(dve_yn, o + 1)
                eng.wait_ge(act_z, o)
                eng.wait_ge(dve_film, sum(s < o + 3 for s in FILM_SLOTS))
                for c in range(C):
                    mm = eng.transpose(bank(B_TY, c * P, P), YN[:, c * P:c * P + P], ident[:, :])
                mm.then_inc(pe_ty, 1)

            def attention(j):
                w = HEAD[j // B]
                eng.wait_ge(act_ek, j + 1)
                eng.wait_ge(act_v, j + 1)
                eng.wait_ge(dve_yr, j)
                v = with_ones(j // B, j)
                for c in range(C):
                    for f in range(0, P, w):
                        mm = eng.matmul(PS[f:f + w, B_ATT, c * (w + 1):(c + 1) * (w + 1)],
                                        EK[:, c * P + f:c * P + f + w], v[:, (c * P + f) // w, :],
                                        start=True, stop=True, tile_position=(0, f))
                mm.then_inc(pe_att, 1)

            def mix(j):
                eng.wait_ge(act_eq, j + 1)
                eng.wait_ge(dve_att, j + 1)
                W = P + Q
                for c in range(C):
                    mm = eng.matmul(bank(B_ATT + c // 2, (c % 2) * W, W), EQ[:, c * P:c * P + P],
                                    ATT[:, c // 2, (c % 2) * W:(c % 2 + 1) * W], start=True, stop=True)
                mm.then_inc(pe_y, 1)

            def output(o):
                l = o // B
                eng.wait_ge(act_hh, o + 1)
                eng.wait_ge(dve_hl, o + 1)
                eng.wait_ge(dve_v, min(o + 4, NT))
                if o == NT - 3:
                    eng.wait_ge(dve_x, o)
                hs = [lambda c: HH[:, c * P:c * P + P], lambda c: HL[:, c * P:c * P + P]]
                ws = [lambda c: WH[3][:, c, :], lambda c: WL[3][:, c, :]]
                split_product(bank(bank_out(o)), hs, ws, fresh=(4 * l + 3 if o % B == 0 else None)).then_inc(pe_o, 1)

            def turn_x(m):
                eng.wait_ge(dve_xn, m + 1)
                eng.wait_ge(act_xf, m)
                if m >= 4:
                    eng.wait_ge(act_ek, m - 3)
                for cc in range(2):
                    for t in range(2):
                        mm = eng.transpose(bank(B_XK, cc * PAIR + t * T, T), XN[:, t, cc * P:cc * P + P], ident[:, :])
                mm.then_inc(pe_a, 1)

            def conditioning(n):
                l, a, k = FILM_STEPS[n]
                eng.wait_ge(ld_film[n], 16)
                eng.wait_ge(dve_cond, 2)
                eng.wait_ge(dve_q, FILM_SLOTS[n])
                w = FILM0[:, :, a:a + k] if l == 0 else FILM1
                for c in range(EC):
                    g = c % 4
                    mm = eng.matmul(PS[g * B:(g + 1) * B, B_Q, 0:k], CT[:, c, :], w[:, c, :],
                                    start=(c < 4), stop=(c >= EC - 4), tile_position=(0, g * B))
                mm.then_inc(pe_film, 1)

            def conditioning_fold(n):
                eng.wait_ge(act_cp, n + 1)
                eng.wait_ge(act_z, max(FILM_SLOTS[n] - 2, 0))
                for c in range(FILM_STEPS[n][2] // P):
                    mm = eng.matmul(bank(B_TY, c * B, B), CP[:, c * P:c * P + P], FOLD[:, :], start=True, stop=True)
                mm.then_inc(pe_fold, 1)

            eng.wait_ge(pool_const, 5)
            eng.wait_ge(ld_vec, 16)
            n = 2 * VROWS
            eng.transpose(bank(B_TY, 0, n), VR, ident[0:n, 0:n]).then_inc(pe_vec, 1)
            turn_x(0)
            turn_x(1)
            for s in SLOTS:
                i, j, o, m = s, s - 2, s - 3, s + 2
                if 0 <= i < NT:
                    keys(i)
                if s in FILM_SLOTS:
                    conditioning(FILM_SLOTS.index(s))
                if 0 <= j < NT:
                    turn_keys(j)
                    turn_queries(j)
                if 0 <= o < NT:
                    turn_y(o)
                if 0 <= i < NT:
                    values(i)
                if 0 <= j < NT:
                    attention(j)
                if 1 <= s and m < NSTEP:
                    turn_x(m)
                if s == 0:
                    eng.wait_ge(dve_mask_rows, 1)
                    for l in range(2):
                        mm = eng.transpose(bank(B_TY, (EC + l) * B, B), MT if l == 0 else MF, ident[0:B, 0:B])
                    mm.then_inc(pe_valid, 1)
                if s in FILM_SLOTS:
                    conditioning_fold(FILM_SLOTS.index(s))
                if 0 <= i < NT:
                    queries(i)
                if s == 0:
                    turn_x(m)
                if s == 0:
                    eng.wait_ge(dve_valid, 1)
                    eng.matmul(bank(B_TQ, 0, B), ones, VALID[0][:, :], start=True, stop=True).then_inc(pe_count, 1)
                    eng.wait_ge(dve_cond, 1)
                    for k in range(EC):
                        mm = eng.transpose(bank(B_TY, k * B, B), COND[:, k * P:k * P + P], ident[0:B, 0:B])
                    mm.then_inc(pe_cond, 1)
                if 0 <= j < NT:
                    mix(j)
                if 0 <= o < NT:
                    output(o)
            for stage, n in DRAIN:
                if stage == "turn":
                    turn_keys(n)
                    turn_queries(n)
                elif stage == "attention":
                    attention(n)
                elif stage == "mix":
                    mix(n)
                elif stage == "turn_y":
                    turn_y(n)
                elif stage == "output":
                    output(n)

        @block.vector
        def _(eng):
            own = [0]

            def then(ins):
                own[0] += 1
                ins.then_inc(dve_own, 1)
                eng.wait_ge(dve_own, own[0])

            def stat_x(n):
                if n < B:
                    if n in [a for a, _ in XLOADS]:
                        eng.wait_ge(ld_x[x_load_of(n)], 16)
                else:
                    eng.wait_ge(dve_x, n - B + 1)
                then(eng.bn_stats(BNX[:, :], X[:, n % B, :]))
                if n >= RING:
                    eng.wait_ge(pool_x, n - RING + 1)
                eng.bn_aggr(MVX[:, n % RING, :], BNX[:, :]).then_inc(dve_stat, 1)
                eng.wait_ge(dve_stat, n + 1)

            def norm_x(m):
                g, p = divmod(m, 2)
                eng.wait_ge(pool_x, 2 * g + 2)
                eng.wait_ge(pe_a, m)
                for t in range(2):
                    n = 2 * g + t
                    r = n % RING
                    ins = eng.tensor_scalar(XN[:, t, :], X[:, n % B, 2 * p * P:2 * (p + 1) * P], MVX[:, r, 0:1],
                                            RSX[:, r:r + 1], ALU.subtract, ALU.mult)
                ins.then_inc(dve_xn, 1)

            def x_low(m):
                g, p = divmod(m, 2)
                eng.wait_ge(act_xh, m + 1)
                if g >= 2:
                    eng.wait_ge(pe_q, 2 * g - 2)
                dst = slice(2 * p, 2 * p + 2)
                eng.tensor_tensor(XL[g % 2][:, dst, :], XF[:, :, :], XH[g % 2][:, dst, :].bitcast(F32),
                                  ALU.subtract).then_inc(dve_xl, 1)

            def keys(i):
                l, g, p = i // B, i // 2, i % 2
                eng.wait_ge(pe_k, i + 1)
                eng.wait_ge(pool_mb, g + 1)
                if g >= 2:
                    eng.wait_ge(pe_tk, 2 * g - 2)
                sk = SK[g % 2][:, 2 * p:2 * p + 2, :]
                then(eng.tensor_tensor(sk, PS[:, B_K, :].rearrange("p (c n) -> p c n", c=2),
                                       MB[g % 2][:, :].unsqueeze(1).to_broadcast([P, 2, PAIR]), ALU.add))
                then(eng.tensor_reduce(KM[:, :, :].rearrange("p c t -> p (c t)"),
                                       sk.rearrange("p c (t n) -> p (c t) n", t=2), AX.X, ALU.max))
                bk = vec(l, "bk", 2 * p, 2)
                then(eng.tensor_tensor(KB[:, :, :], KM[:, :, :], bk.unsqueeze(2).to_broadcast([P, 2, 2]), ALU.add))
                for cc in range(2):
                    half_sk = sk[:, cc, :].rearrange("p (t n) -> p t n", t=2)
                    ins = eng.scalar_tensor_tensor(
                        out=half_sk, in0=half_sk, scalar=bk[:, cc:cc + 1],
                        in1=KB[:, cc, :].unsqueeze(2).to_broadcast([P, 2, T]), op0=ALU.add, op1=ALU.subtract)
                ins.then_inc(dve_ks, 1)

            def queries(i):
                w = HEAD[i // B]
                eng.wait_ge(pe_q, i + 1)
                if i % B == 0:
                    eng.wait_ge(ld_bias[3 * (i // B) + 1], 16)
                if i >= 2:
                    eng.wait_ge(pe_tq, i - 1)
                eng.tensor_tensor(SQ[i % 2][:, :], PS[:, B_Q, :], BB[:, 1, :], ALU.add).then_inc(dve_q, 1)
                eng.wait_ge(dve_q, i + 1)
                sq = SQ[i % 2][:, :].rearrange("p (h n) -> p h n", n=w)
                eng.wait_ge(pool_q, i)
                eng.tensor_reduce(QM[:, 0:D // w], sq, AX.X, ALU.max).then_inc(dve_qm, 1)

            def values(i):
                eng.wait_ge(pe_v, i + 1)
                if i % B == 0:
                    eng.wait_ge(ld_bias[3 * (i // B)], 16)
                if i >= 3:
                    eng.wait_ge(pe_att, i - 2)
                w = HEAD[i // B]
                eng.tensor_tensor(with_ones(i // B, i)[:, :, 1:], PS[:, B_VO, :].rearrange("p (h n) -> p h n", n=w),
                                  BB[:, 0, :].rearrange("p (h n) -> p h n", n=w), ALU.add).then_inc(dve_v, 1)

            def heads(j):
                l = j // B
                w = HEAD[l]
                eng.wait_ge(pe_att, j + 1)
                eng.wait_ge(pe_y, j)
                if j == B:
                    for h in range(P // w):
                        ATT_h = ATT[h * w:(h + 1) * w, :, :]
                        eng.memset(ATT_h[:, :, 2 * h:2 * h + 2], 1.0)
                        eng.memset(ATT_h[:, :, 2 * P + Q + 2 * h:2 * P + Q + 2 * h + 2], 1.0)
                ps = PS[:, B_ATT, 0:C * (w + 1)].rearrange("p (c n) -> p c n", c=C)
                then(eng.reciprocal(RK[:, :, :], ps[:, :, 0:1]))
                dst = ATT[:, :, Q:Q + 2 * P].rearrange("p b (c n) -> p b c n", c=2)
                if l == 0:
                    then(eng.tensor_tensor(AB[:, :, :], ps[:, :, 1:], RK[:, :, :].to_broadcast([P, C, w]), ALU.mult))
                for a in range(0, P, w):
                    own_block = dst[a:a + w, :, :, a:a + w]
                    if l == 0:
                        ins = eng.transpose(own_block, AB[a:a + w, :, :].rearrange("p (b c) n -> p b c n", b=2))
                    else:
                        ins = eng.tensor_tensor(own_block,
                                                ps[a:a + w, :, 1:].rearrange("p (b c) n -> p b c n", b=2),
                                                RK[a:a + w, :, :].rearrange("p (b c) n -> p b c n", b=2)
                                                .to_broadcast([w, 2, 2, w]), ALU.mult)
                ins.then_inc(dve_att, 1)

            def mixed(j):
                eng.wait_ge(pe_y, j + 1)
                ps = PS[:, B_ATT:B_ATT + 2, 0:Q]
                sums = bass.AP(tensor=ps.tensor, offset=ps.offset, ap=[ps.ap[0], ps.ap[1], [Q + 2 * P, 2], [1, Q]])
                then(eng.reciprocal(RQ[:, :].rearrange("p (b s q) -> p b s q", b=2, s=2), sums))
                eng.wait_ge(pe_ty, j)
                eng.tensor_tensor(YN[:, :].rearrange("p (b h n) -> p b h n", b=2, n=32),
                                  PS[:, B_ATT:B_ATT + 2, Q:Q + 2 * P].rearrange("p b (h n) -> p b h n", n=32),
                                  RQ[:, :].rearrange("p (b h) -> p b h", b=2).unsqueeze(3).to_broadcast([P, 2, 8, 32]),
                                  ALU.mult).then_inc(dve_yr, 1)
                eng.wait_ge(dve_yr, j + 1)
                then(eng.bn_stats(BNY[:, :], YN[:, :]))
                eng.wait_ge(pool_y, j)
                eng.bn_aggr(MVY[:, :], BNY[:, :]).then_inc(dve_ystat, 1)

            def norm_y(j):
                eng.wait_ge(dve_ystat, j + 1)
                eng.wait_ge(pool_y, j + 1)
                eng.tensor_scalar(YN[:, :], YN[:, :], MVY[:, 0:1], RSY[:, :], ALU.subtract, ALU.mult)\
                   .then_inc(dve_yn, 1)

            def h_mul(o):
                eng.wait_ge(act_t, o + 1)
                eng.scalar_tensor_tensor(out=H[:, :], in0=H[:, :], scalar=1.0, in1=Z[:, :],
                                         op0=ALU.add, op1=ALU.mult).then_inc(dve_h, 1)

            def h_low(o):
                eng.wait_ge(act_hh, o + 1)
                eng.wait_ge(dve_h, o + 1)
                eng.wait_ge(pe_o, o)
                eng.tensor_tensor(HL[:, :], H[:, :], HH[:, :].bitcast(F32), ALU.subtract).then_inc(dve_hl, 1)

            def add_x(o):
                eng.wait_ge(pe_o, o + 1)
                b = o % B
                eng.wait_ge(pool_bo, o + 1)
                eng.tensor_tensor(X[:, b, :], PS[:, bank_out(o), :], X[:, b, :], ALU.add).then_inc(dve_x, 1)

            def conditioning(n):
                l, a, k = FILM_STEPS[n]
                c0, cn = a % D // P, k // P
                eng.wait_ge(pe_fold, n + 1)
                ps = PS[:, B_TY, 0:cn * B].rearrange("p (c b) -> p c b", c=cn)
                here = slice(c0, c0 + cn)

                def wide(v):
                    return v.unsqueeze(2).to_broadcast([P, cn, B])

                if a < D:
                    then(eng.scalar_tensor_tensor(out=G[:, here, :], in0=ps, scalar=1.0,
                                                  in1=wide(vec(l, "film_b", c0, cn)), op0=ALU.add, op1=ALU.add))
                    last = eng.scalar_tensor_tensor(out=FA[l][:, here, :], in0=G[:, here, :], scalar=0.5,
                                                    in1=wide(vec(l, "film_scale", c0, cn)), op0=ALU.mult, op1=ALU.mult)
                else:
                    then(eng.tensor_tensor(U[:, here, :], ps, wide(vec(l, "film_b", C + c0, cn)), ALU.add))
                    then(eng.tensor_tensor(G[:, here, :], G[:, here, :], wide(vec(l, "film_bias", c0, cn)), ALU.mult))
                    then(eng.tensor_tensor(G[:, here, :], G[:, here, :], U[:, here, :], ALU.add))
                    last = eng.tensor_scalar(FC[l][:, here, :], G[:, here, :], 0.5, None, ALU.mult)
                last.then_inc(dve_film, 1)

            def start():
                eng.wait_ge(pool_const, 5)
                for g in range(Q):
                    a, z = 32 * g, 32 * g + 32
                    eng.memset(ATT[a:z, :, g:g + 1], 1.0)
                    eng.memset(ATT[a:z, :, 2 * P + Q + g:2 * P + Q + g + 1], 1.0)
                eng.tensor_reduce(FOLD[:, :], ident[:, :].rearrange("p (g b) -> p b g", b=B), AX.X, ALU.add)

            def start_masks():
                eng.wait_ge(ld_mask, 32)
                eng.tensor_scalar(MT, MI, 1.0, None, ALU.not_equal).then_inc(dve_mask_rows, 1)

            def start_valid():
                eng.wait_ge(pe_valid, 1)
                eng.tensor_copy(VALID[1][:, :], PS[:, B_TY, (EC + 1) * B:(EC + 2) * B])
                eng.tensor_copy(VALID[0][:, :], PS[:, B_TY, EC * B:(EC + 1) * B]).then_inc(dve_valid, 1)

            def start_cond():
                eng.wait_ge(act_cond, 2)
                for n in range(2):
                    half_c = COND[:, n * D:n * D + D]
                    ins = eng.scalar_tensor_tensor(out=half_c, in0=CTH[n], scalar=1.0, in1=half_c,
                                                   op0=ALU.add, op1=ALU.mult)
                ins.then_inc(dve_cond, 1)

            def start_count():
                eng.wait_ge(pe_count, 1)
                u = U[:, 0, :]
                then(eng.tensor_scalar(u, PS[:, B_TQ, 0:B], 0.0, HUGE, ALU.is_equal, ALU.mult))
                then(eng.tensor_scalar(u, u, HUGE, 0.0, ALU.mult, ALU.mult))
                eng.wait_ge(dve_valid, 1)
                eng.tensor_tensor(VALID[0][:, :], VALID[0][:, :], u, ALU.add).then_inc(dve_mask, 1)
                eng.wait_ge(pe_cond, 1)
                eng.tensor_scalar(CT[:, :, :], PS[:, B_TY, 0:EC * B].rearrange("p (k b) -> p k b", k=EC), 0.5, None,
                                  ALU.mult).then_inc(dve_cond, 1)

            start()
            stat_x(0)
            stat_x(1)
            eng.wait_ge(pe_vec, 1)
            eng.tensor_copy(VC[:, :], PS[:, B_TY, 0:2 * VROWS]).then_inc(dve_vec, 1)
            norm_x(0)
            norm_x(1)
            x_low(0)
            split_low(eng, 0, range(2))
            x_low(1)
            split_low(eng, 0, range(2, C))
            start_masks()
            split_low(eng, 1, LOW_ON_DVE[1])
            stat_x(2)
            stat_x(3)
            start_cond()
            for s in SLOTS:
                i, j, o, m = s, s - 2, s - 3, s + 2
                if 0 < s and m < NSTEP:
                    norm_x(m)
                if 0 <= i < NT:
                    keys(i)
                if s == 0:
                    split_low(eng, 2, LOW_ON_DVE[2])
                    values(i)
                    norm_x(m)
                    start_valid()
                    start_count()
                for n in stats_at(s):
                    stat_x(n)
                if 0 <= o < NT:
                    h_mul(o)
                for w in SPLIT_MID.get(s, []):
                    split_low(eng, w, LOW_ON_DVE[w])
                if 1 <= i < NT:
                    values(i)
                if 0 <= j < NT:
                    heads(j)
                if 0 <= o < NT:
                    h_low(o)
                if 0 < s and m < NSTEP:
                    x_low(m)
                if s in FILM_SLOTS:
                    conditioning(FILM_SLOTS.index(s))
                if 0 <= j < NT:
                    mixed(j)
                if 0 <= i < NT:
                    queries(i)
                for w in SPLIT_LATE.get(s, []):
                    split_low(eng, w, LOW_ON_DVE[w])
                if s == 0:
                    x_low(m)
                if 0 <= o < NT:
                    add_x(o)
                if 0 <= j < NT:
                    norm_y(j)
                for w in SPLIT_END.get(s, []):
                    split_low(eng, w, LOW_ON_DVE[w])
            for stage, n in DRAIN:
                if stage == "heads":
                    heads(n)
                elif stage == "y":
                    mixed(n)
                elif stage == "norm_y":
                    norm_y(n)
                elif stage == "h":
                    h_mul(n)
                elif stage == "h_low":
                    h_low(n)
                elif stage == "add_x":
                    add_x(n)


def kernel(**inputs):
    import numpy as np
    import concourse.bacc as bacc
    from concourse.bass_utils import run_bass_kernel_spmd

    a = {k: np.asarray(v) for k, v in inputs.items()}
    n0, n1 = "L0_cond_", "L1_cond_"
    names = [
        dict(norm_scale="norm_scale", norm_bias="norm_bias", bk="bk", film_scale="film_norm_scale",
             film_bias="film_norm_bias", film_b="film_emb_b", bv="bv", bq="bq", bo="film_out_b",
             k="Wk", v="Wv", q="Wq", o="film_out_W", film="film_emb_W"),
        dict(norm_scale="ln_w", norm_bias="ln_b", bk="bk", film_scale="ln2_w", film_bias="ln2_b",
             film_b="b_emb", bv="bv", bq="bq", bo="b_out", k="Wk", v="Wv", q="Wq", o="W_out", film="W_emb"),
    ]
    got = [{k: a[p + v] for k, v in n.items()} for p, n in zip((n0, n1), names)]
    arrays = {
        "x": a["x"], "cond": a["cond_2048"],
        "mask0": a["mask_BxS_ik0"], "mask1": a["mask_BxSx1_fk1"].reshape(a["mask_BxS_ik0"].shape),
        "vec_rows": np.concatenate([g[v] for g in got for v in VECTORS]).reshape(-1, P),
        "bias_rows": np.stack([g[v] for g in got for v in ("bv", "bq", "bo")]),
    }
    for l, g in enumerate(got):
        for m in MATS:
            arrays[f"w{m}{l}"] = g[m]
        arrays[f"film{l}"] = g["film"]
    nc = bacc.Bacc("TRN2", target_bir_lowering=False, num_devices=1)
    arrays = {f"in_{k}": np.ascontiguousarray(v) for k, v in arrays.items()}
    ap = {k[3:]: nc.dram_tensor(k, v.shape, mybir.dt.from_np(v.dtype), kind="ExternalInput").ap()
          for k, v in arrays.items()}
    out = nc.dram_tensor("out_x", a["x"].shape, F32, kind="ExternalOutput").ap()
    build_blocks(nc, ap["x"], ap["cond"], ap["mask0"], ap["mask1"],
                 [[ap[f"w{m}{l}"] for m in MATS] for l in range(2)], [ap["film0"], ap["film1"]],
                 ap["vec_rows"], ap["bias_rows"], out)
    r = run_bass_kernel_spmd(nc, [arrays], core_ids=[0])
    return r.results[0]["out_x"]
```
